# Optimizing a Trainium2 kernel written in Bass

```python
import numpy as np
import jax
import jax.numpy as jnp

def _softmax(x, axis=-1):
    return jax.nn.softmax(x, axis=axis)

def _gelu(x):
    return jax.nn.gelu(x, approximate=True)

def _silu(x):
    return jax.nn.silu(x)

def _sigmoid(x):
    return jax.nn.sigmoid(x)

def _layernorm(x, axis=-1, eps=1e-05):
    m = jnp.mean(x, axis=axis, keepdims=True)
    v = jnp.var(x, axis=axis, keepdims=True)
    return (x - m) / jnp.sqrt(v + eps)

def _scatter_add(tgt, idx, src, axis=0):
    return tgt.at[idx].add(src)

def _segment_sum(src, seg, n):
    return jax.ops.segment_sum(src, seg, n)
kernel_name = 'mk_gnn_preln_d2_gnn_r64_07f486'

def setup_inputs(seed: int=0):
    np.random.seed(seed)
    _w = jnp.asarray

    def _rec_inputs():
        import jax
        import jax.numpy as jnp
        _gk = jax.random.key(seed)
        x = -0.0003713 + 1 * jax.random.normal(jax.random.fold_in(_gk, 1), (50000, 256), jnp.float32)
        _s = jax.random.randint(jax.random.fold_in(_gk, 2), (12500,), 0, 50000, jnp.int32)
        _d = jax.random.randint(jax.random.fold_in(_gk, 3), (12500,), 0, 50000, jnp.int32)
        _loop = jnp.arange(50000, dtype=jnp.int32)
        src = jnp.concatenate([_s, _d, _loop])
        dst = jnp.concatenate([_d, _s, _loop])
        _o = jnp.argsort(dst, stable=True)
        src = src[_o]
        dst = dst[_o]
        return (x, src, dst)
    x, src, dst = _rec_inputs()

    def _L0_gnn_setup():
        import jax, jax.numpy as jnp
        import numpy as np
        N = 50000
        E = 3125
        H = 8
        C = 256
        IN = 256
        NEG_SLOPE = 0.2
        EPS = 1e-16
        key = jax.random.key(seed)
        k1, k2, k3, k4, k5, k6 = jax.random.split(key, 6)
        glorot = lambda k, shape, fan: jax.random.normal(k, shape, jnp.float32) * np.sqrt(2.0 / fan)
        x = jax.random.normal(k1, (N, IN), jnp.float32)
        edge_index = jax.random.randint(k2, (2, E), 0, N, jnp.int32)
        W = glorot(k3, (IN, H * C), IN + H * C)
        att_src = glorot(k4, (H, C), C)
        att_dst = glorot(k5, (H, C), C)
        bias = jnp.zeros((C,), jnp.float32)
        return {'x': x, 'edge_index': edge_index, 'W': W, 'att_src': att_src, 'att_dst': att_dst, 'bias': bias}
    _L0_gnn_all = _L0_gnn_setup()
    _L0_gnn_in = {k: v for k, v in _L0_gnn_all.items() if k in ('W', 'att_src', 'att_dst', 'bias')}
    del _L0_gnn_all

    def _L1_gnn_setup():
        import jax, jax.numpy as jnp
        import numpy as np
        N, E, H, D, P = (50000, 12500, 4, 64, 16)
        IN = 256
        key = jax.random.key(seed)
        ks = jax.random.split(key, 8)
        feat = jax.random.normal(ks[0], (N, IN), jnp.float32)
        src = jax.random.randint(ks[1], (E,), 0, N, dtype=jnp.int32)
        dst = jax.random.randint(ks[2], (E,), 0, N, dtype=jnp.int32)
        C = IN - P
        W = jax.random.normal(ks[3], (C, H * D), jnp.float32) / np.sqrt(C).astype(np.float32)
        attn_src = jax.random.normal(ks[4], (1, H, D), jnp.float32) * 0.1
        attn_dst = jax.random.normal(ks[5], (1, H, D), jnp.float32) * 0.1
        pos_attn_src = jax.random.normal(ks[6], (1, H, P), jnp.float32) * 0.1
        pos_attn_dst = jax.random.normal(ks[7], (1, H, P), jnp.float32) * 0.1
        return dict(feat=feat, src=src, dst=dst, W=W, attn_src=attn_src, attn_dst=attn_dst, pos_attn_src=pos_attn_src, pos_attn_dst=pos_attn_dst)
    _L1_gnn_all = _L1_gnn_setup()
    _L1_gnn_in = {k: v for k, v in _L1_gnn_all.items() if k in ('W', 'attn_src', 'attn_dst', 'pos_attn_src', 'pos_attn_dst')}
    del _L1_gnn_all
    return {'x': x, 'src': src, 'dst': dst, 'L0_gnn_W': _L0_gnn_in['W'], 'L0_gnn_att_src': _L0_gnn_in['att_src'], 'L0_gnn_att_dst': _L0_gnn_in['att_dst'], 'L0_gnn_bias': _L0_gnn_in['bias'], 'L1_gnn_W': _L1_gnn_in['W'], 'L1_gnn_attn_src': _L1_gnn_in['attn_src'], 'L1_gnn_attn_dst': _L1_gnn_in['attn_dst'], 'L1_gnn_pos_attn_src': _L1_gnn_in['pos_attn_src'], 'L1_gnn_pos_attn_dst': _L1_gnn_in['pos_attn_dst']}

def reference(x, src, dst, L0_gnn_W, L0_gnn_att_src, L0_gnn_att_dst, L0_gnn_bias, L1_gnn_W, L1_gnn_attn_src, L1_gnn_attn_dst, L1_gnn_pos_attn_src, L1_gnn_pos_attn_dst):
    import jax
    import jax.numpy as jnp

    def _L0_gnn_ref(x, edge_index, W, att_src, att_dst, bias):
        import jax, jax.numpy as jnp
        import numpy as np
        N = 50000
        E = 3125
        H = 8
        C = 256
        IN = 256
        NEG_SLOPE = 0.2
        EPS = 1e-16
        h = (x @ W).reshape(N, H, C)
        a_src = jnp.einsum('nhc,hc->nh', h, att_src)
        a_dst = jnp.einsum('nhc,hc->nh', h, att_dst)
        src, dst = (edge_index[0], edge_index[1])
        e = jax.nn.leaky_relu(a_src[src] + a_dst[dst], NEG_SLOPE)
        m = jax.ops.segment_max(e, dst, num_segments=N)
        e = jnp.exp(e - m[dst])
        denom = jax.ops.segment_sum(e, dst, num_segments=N)
        alpha = e / (denom[dst] + EPS)
        msg = h[src] * alpha[:, :, None]
        out = jax.ops.segment_sum(msg, dst, num_segments=N)
        return out.mean(axis=1) + bias

    def _L1_gnn_ref(feat, src, dst, W, attn_src, attn_dst, pos_attn_src, pos_attn_dst):
        import jax, jax.numpy as jnp
        import numpy as np
        N, E, H, D, P = (50000, 12500, 4, 64, 16)
        IN = 256
        content = feat[:, :-P]
        pos = feat[:, -P:]
        ft = (content @ W).reshape(N, H, D)
        s_src = jnp.einsum('nhd,hd->nh', ft, attn_src[0])
        s_dst = jnp.einsum('nhd,hd->nh', ft, attn_dst[0])
        p_src = jnp.einsum('np,hp->nh', pos, pos_attn_src[0])
        p_dst = jnp.einsum('np,hp->nh', pos, pos_attn_dst[0])
        e = (s_src + p_src)[src] + (s_dst + p_dst)[dst]
        e = jax.nn.leaky_relu(e, negative_slope=0.2)
        emax = jax.ops.segment_max(e, dst, num_segments=N)
        ex = jnp.exp(e - emax[dst])
        denom = jax.ops.segment_sum(ex, dst, num_segments=N)
        a = ex / denom[dst]
        msg = ft[src] * a[:, :, None]
        out = jax.ops.segment_sum(msg, dst, num_segments=N)
        h = out.reshape(N, H * D)
        return h + feat
    edge_index = jnp.stack([src, dst])
    h = jnp.maximum(_layernorm(x, axis=-1), 0.0)
    x = x + _L0_gnn_ref(h, edge_index, L0_gnn_W, L0_gnn_att_src, L0_gnn_att_dst, L0_gnn_bias)
    h = jnp.maximum(_layernorm(x, axis=-1), 0.0)
    x = x + _L1_gnn_ref(h, src, dst, L1_gnn_W, L1_gnn_attn_src, L1_gnn_attn_dst, L1_gnn_pos_attn_src, L1_gnn_pos_attn_dst)
    return x

_drawn_inputs = setup_inputs


def setup_inputs(seed=0):
    import zlib

    import numpy as np

    out = dict(_drawn_inputs(seed))
    spreads = {'L0_gnn_bias': (0.0, 0.1)}
    factors = {'L0_gnn_att_src': 7.597,
     'L0_gnn_att_dst': 8.0,
     'L1_gnn_attn_dst': 4.521,
     'L1_gnn_pos_attn_src': 3.015,
     'L1_gnn_pos_attn_dst': 6.253}
    for name, (base, spread) in spreads.items():
        noise = np.random.default_rng([zlib.crc32(name.encode()), seed]).standard_normal(out[name].shape)
        drawn = base * np.exp(spread * noise) if base else spread * noise
        out[name] = jnp.asarray(drawn.astype(out[name].dtype))
    for name, factor in factors.items():
        out[name] = (out[name] * factor).astype(out[name].dtype)
    return out
```

```python
import concourse.bass as bass
from concourse import mybir
from contextlib import ExitStack

F32 = mybir.dt.float32
F32R = mybir.dt.float32r
I32 = mybir.dt.int32
ALU = mybir.AluOpType
ACT = mybir.ActivationFunctionType
AX = mybir.AxisListType

P = 128
EPS = 1e-5
SLOPE = 0.2
NONE = 60000
LOW = -1e30
BANK = 512

EDGE_COLS = 14
HEADS_AT = EDGE_COLS * P
SPARE = HEADS_AT + P
PARTS = 3
LIST_PADS = PARTS + 1
BATCH = 5
LAG = 2
SLOTS = 3


def last(ap, n):
    return ap.rearrange("p (m o) -> p m o", o=1).broadcast_to([ap.shape[0], ap.shape[1], n])


def held(eng, sem, value, mark):
    eng.wait_ge(sem, value)
    eng.sem_inc(mark, 1)


def looped(eng, count, body):
    body(0)
    with eng.Fori(1, count) as i:
        body(i)


class Sizes:
    def __init__(s, x, src, W0, att0, W1, attn1, pos1):
        s.N, s.IN = x.shape
        s.E = src.shape[0]
        s.H0, s.C0 = att0.shape
        _, s.H1, s.D1 = attn1.shape
        s.POS = pos1.shape[2]
        s.CON = s.IN - s.POS
        s.W = -(-s.E // P)
        s.LW = -(-s.W // EDGE_COLS) * EDGE_COLS
        s.KC = s.IN // P


def prepare(nc, S, T, lists, src, dst, W0, att0s, att0d, W1, attn_s, attn_d, pos_s, pos_d, bias):
    W, LW, KC, H0, C0 = S.W, S.LW, S.KC, S.H0, S.C0
    full = P - 1
    rest = S.E - full * W
    with ExitStack() as ctx:
        def sb(n, s, d=F32):
            return ctx.enter_context(nc.sbuf_tensor(n, s, d))

        def sem(n):
            return ctx.enter_context(nc.semaphore(n))
        src_i = sb("src_i", [P, W], I32)
        dst_i = sb("dst_i", [P, W], I32)
        src_f = sb("src_f", [P, W])
        dst_f = sb("dst_f", [P, W])
        own = sb("own", [P, W])
        start = sb("start", [P, W])
        low_start = sb("low_start", [P, W + 1])
        keep = sb("keep", [P, W])
        fwd = sb("fwd", [P, W, 1])
        own_count = sb("own_count", [P, W, 1])
        place = sb("place", [P, W])
        shift = [sb(f"shift{i}", [P, W], I32) for i in range(2)]
        moved = sb("moved", [P, W], I32)
        comp_src = sb("comp_src", [P, W])
        comp_dst = sb("comp_dst", [P, W])
        comp_own = sb("comp_own", [P, W])
        ones = sb("ones", [P, W])
        packed = sb("packed", [P, W, 3])
        part = [packed] + [sb(f"part{k}", [P, W, 3]) for k in range(1, PARTS)]
        pads = sb("pads", [LIST_PADS, W * 3])
        upto = sb("upto", [P, P])
        spread = sb("spread", [P, 2, P])
        ones_pp = sb("ones_pp", [P, P])
        ends_row = sb("ends_row", [P, 2, P])
        pick = sb("pick", [P, P])
        share_i = sb("share_i", [P, 1], I32)
        share = sb("share", [P, 1])
        lane0 = sb("lane0", [P, 1])
        begin = sb("begin", [P, PARTS])
        deal = sb("deal", [P, 12])
        begin_i = sb("begin_i", [P, PARTS], I32)
        most = sb("most", [1, 1])
        begun = sb("begun", [1, LW // EDGE_COLS])
        pos_i = sb("pos_i", [P, LW], I32)
        pos_f = sb("pos_f", [P, LW])
        valid = sb("valid", [P, LW])
        spare_i = sb("spare_i", [P, LW], I32)
        spare_f = sb("spare_f", [P, LW])
        lane_i = sb("lane_i", [P, 1], I32)
        lane_f = sb("lane_f", [P, 1])
        head_lane = sb("head_lane", [P, 1])
        empty = sb("empty", [P, 1])
        w0 = sb("w0", [P, KC, H0 * C0])
        out_row_f = sb("out_row_f", [P, LW])
        is_head = sb("is_head", [P, LW])
        linked = sb("linked", [P, P])
        link = sb("link", [P, 1])
        att_b = sb("att_b", [P, H0 * C0])
        prod = sb("prod", [P, H0 * C0])
        tmp = sb("tmp", [P, LW])
        rank_mask = sb("rank_mask", [P, P])
        tail_first = sb("tail_first", [P, 1])
        cross = Cross(nc, ctx, "own", 1)
        loaded = sem("edges_loaded")
        padded = sem("edges_padded")
        weights_loaded = sem("weights_loaded")
        constants = sem("constants")
        upto_set = sem("upto_set")
        att_loaded = sem("att_loaded")
        att_used = sem("att_used")
        ready = sem("rows_ready")
        done = sem("matmuls_done")
        weights_zeroed = sem("weights_zeroed")
        packed_made = sem("packed_made")
        packed_stored = sem("packed_stored")
        begins_made = sem("begins_made")
        parts_in = sem("parts_in")
        block = ctx.enter_context(nc.Block())

        @block.sync
        def _(sp):
            sp.dma_start(w0[:, :, :], W0.rearrange("(k p) n -> p k n", p=P)).then_inc(weights_loaded, 16)
            sp.dma_start(T.bias_b[:, :], bias.partition_broadcast(P)).then_inc(weights_loaded, 16)
            sp.wait_ge(weights_zeroed, 1)
            top = S.CON - P
            sp.dma_start(T.r1[:, 0, 0:S.IN], W1[0:P, :]).then_inc(weights_loaded, 16)
            sp.dma_start(T.r1[0:top, 1, 0:S.IN], W1[P:S.CON, :]).then_inc(weights_loaded, 16)
            for k, pos in enumerate((pos_s, pos_d)):
                c = S.IN + k * S.H1
                sp.dma_start(T.r1[top:P, 1, c:c + S.H1], pos[0].rearrange("h p -> p h"),
                             allow_slow_non_contiguous=True).then_inc(weights_loaded, 16)
            sp.wait_ge(padded, 2)
            for tile, dram in ((src_i, src), (dst_i, dst)):
                rows = dram[0:full * W].rearrange("(p w) -> p w", w=W)
                for a, b in ((0, 112), (112, full)):
                    sp.dma_start(tile[a:b, :], rows[a:b, :]).then_inc(loaded, 16)
                sp.dma_start(tile[full:P, 0:rest],
                             dram[full * W:S.E].rearrange("(o w) -> o w", o=1)).then_inc(loaded, 16)
            sp.wait_ge(packed_made, 1)
            sp.dma_start(lists[0:P * W, :].rearrange("(p w) c -> p (w c)", w=W),
                         packed[:, :, :].rearrange("p w c -> p (w c)")).then_inc(packed_stored, 16)
            sp.dma_start(lists[P * W:(P + LIST_PADS) * W, :].rearrange("(p w) c -> p (w c)", w=W),
                         pads[:, :]).then_inc(packed_stored, 16)
            for k, (vec, n) in enumerate(((att0s, H0 * C0), (att0d, H0 * C0), (attn_s, S.IN), (attn_d, S.IN))):
                if k:
                    sp.wait_ge(att_used, k)
                sp.dma_start(att_b[:, 0:n], vec.partition_broadcast(P)).then_inc(att_loaded, 16)
            sp.wait_ge(att_loaded, 64)
            sp.wait_ge(loaded, 96)
            sp.wait_ge(weights_loaded, 96)

        @block.gpsimd
        def _(pool):
            pool.memset(T.ident[:, :], 0.0).then_inc(constants, 1)
            pool.memset(rank_mask[:, :], 1.0).then_inc(constants, 1)
            pool.wait_ge(constants, 2)
            pool.affine_select(out=T.ident[:, :], in_=T.ident[:, :], compare_op=ALU.not_equal, fill=1.0,
                               base=0, pattern=[[-1, P]], channel_multiplier=1).then_inc(constants, 1)
            pool.affine_select(out=rank_mask[:, :], in_=rank_mask[:, :], compare_op=ALU.is_gt, fill=0.0,
                               base=0, pattern=[[-1, P]], channel_multiplier=1).then_inc(constants, 1)
            pool.iota(pos_i[:, :], [[1, LW]], 0, channel_multiplier=0).then_inc(constants, 1)
            pool.iota(spare_i[:, :], [[0, LW // EDGE_COLS], [P, EDGE_COLS]], S.N, channel_multiplier=1).then_inc(constants, 1)
            pool.iota(lane_i[:, :], [[1, 1]], S.N, channel_multiplier=1).then_inc(constants, 1)
            pool.memset(upto[:, :], 1.0).then_inc(upto_set, 1)
            pool.wait_ge(upto_set, 1)
            pool.affine_select(out=upto[:, :], in_=upto[:, :], compare_op=ALU.is_ge, fill=0.0,
                               base=0, pattern=[[1, P]], channel_multiplier=-1).then_inc(constants, 1)
            pool.wait_ge(packed_stored, 32)
            pool.wait_ge(begins_made, 1)
            for k in range(PARTS):
                pool.indirect_dma_start(
                    out=part[k][:, :, :].rearrange("p w c -> p (w c)"), out_offset=None,
                    in_=lists.rearrange("n c -> (n c)").rearrange("(n o) -> n o", o=1),
                    in_offset=bass.IndirectOffsetOnAxis(ap=begin_i[:, k:k + 1], axis=0),
                    bounds_check=(P + LIST_PADS) * W * 3 - 1, oob_is_err=False).then_inc(parts_in, 16)

        @block.tensor
        def _(te):
            te.wait_ge(constants, 8)
            cross.keys_pe(T.psum, T.ident, ready, done, 1)
            cross.sums_pe(T.psum, ready, done, 2)
            te.wait_ge(ready, 3)
            nc.tensor.matmul(T.psum[:, 4, 0:2 * P], ones_pp[:, :], spread[:, :, :],
                             start=True, stop=True).then_inc(done, 1)
            te.wait_ge(ready, 4)
            nc.tensor.matmul(T.psum[:, 5, 0:1], ones_pp[:, :], deal[:, 8:9], start=True, stop=True).then_inc(done, 1)
            te.wait_ge(ready, 5)
            nc.tensor.transpose(T.psum[0:1, 0, 0:P], T.count[:, :], T.ident[:, :]).then_inc(done, 1)
            T.cross.keys_pe(T.psum, T.ident, ready, done, 6)

        @block.vector
        def _(v):
            v.memset(src_i[:, :], NONE).then_inc(padded, 1)
            v.memset(dst_i[:, :], NONE).then_inc(padded, 1)
            v.memset(T.r1[:, :, :], 0.0).then_inc(weights_zeroed, 1)
            v.memset(T.eps[:, :], EPS)
            v.memset(ones[:, :], 1.0)
            v.memset(ones_pp[:, :], 1.0)
            v.memset(pads[:, :], 0.0)
            v.memset(T.src[:, LW:], 0)
            v.memset(T.dst[:, LW:], 0)
            v.memset(T.low_start[:, LW:], 0.0)
            v.memset(T.low_pad[:, LW:], LOW)
            v.memset(T.low_own1[:, LW:], LOW)
            v.wait_ge(constants, 8)
            v.tensor_copy(pos_f[:, :], pos_i[:, :])
            v.tensor_copy(lane_f[:, :], lane_i[:, :])
            v.tensor_scalar(head_lane[:, :], lane_i[:, :], float(HEADS_AT), None, ALU.add)
            v.tensor_copy(spare_f[:, :], spare_i[:, :])
            v.wait_ge(loaded, 96)
            v.tensor_copy(src_f[:, :], src_i[:, :])
            v.tensor_copy(dst_f[:, :], dst_i[:, :])
            v.drain()
            v.memset(start[:, 0:1], 0.0)
            v.tensor_tensor(start[:, 1:W], dst_f[:, 1:W], dst_f[:, 0:W - 1], ALU.not_equal)
            v.tensor_tensor(own[:, :], src_f[:, :], dst_f[:, :], ALU.is_equal)
            v.memset(low_start[:, W:W + 1], 0.0)
            v.tensor_copy(cross.keys[:, 0:1], dst_f[:, W - 1:W])
            v.tensor_copy(cross.keys[:, 1:2], dst_f[:, 0:1])
            v.drain()
            v.tensor_scalar(low_start[:, 0:W], start[:, :], LOW, None, ALU.mult)
            v.tensor_scalar(keep[:, :], start[:, :], -1.0, 1.0, ALU.mult, ALU.add)
            v.drain()
            cross.keys_dve(v, T.psum, ready, done, 1)
            v.tensor_copy(fwd[:, :, 0], own[:, :])
            v.drain()
            cross.sums_dve(v, T.psum, fwd, fwd, own_count, keep, low_start, W, ready, done, 2, values=own)
            v.tensor_scalar(tmp[:, 0:W], own[:, :], -1.0, 1.0, ALU.mult, ALU.add)
            v.drain()
            v.tensor_tensor_scan(place[:, :], ones[:, :], tmp[:, 0:W], 0.0, ALU.mult, ALU.add)
            v.drain()
            v.tensor_copy(T.count[:, :], place[:, W - 1:W])
            v.drain()
            v.scalar_tensor_tensor(out=place[:, :], in0=pos_f[:, 0:W], scalar=1.0, in1=place[:, :],
                                   op0=ALU.add, op1=ALU.subtract)
            v.drain()
            v.tensor_tensor(shift[0][:, :], place[:, :], tmp[:, 0:W], ALU.mult)
            v.tensor_copy(comp_src[:, :], src_f[:, :])
            v.tensor_copy(comp_dst[:, :], dst_f[:, :])
            v.tensor_copy(comp_own[:, :], own_count[:, :, 0])
            v.drain()
            bit = 0
            while (1 << bit) < W:
                k = 1 << bit
                a, b = shift[bit % 2], shift[(bit + 1) % 2]
                v.tensor_scalar(moved[:, :], a[:, :], k, None, ALU.bitwise_and)
                v.drain()
                v.scalar_tensor_tensor(out=b[:, :], in0=moved[:, :], scalar=0.0, in1=a[:, :],
                                       op0=ALU.is_equal, op1=ALU.mult)
                v.drain()
                v.copy_predicated(b[:, 0:W - k], moved[:, k:W], a[:, k:W])
                for t in (comp_src, comp_dst, comp_own):
                    v.copy_predicated(t[:, 0:W - k], moved[:, k:W], t[:, k:W])
                v.drain()
                bit += 1
            for k, comp in enumerate((comp_src, comp_dst, comp_own)):
                v.tensor_copy(packed[:, :, k], comp[:, :])
            v.tensor_scalar(spread[:, 0, :], upto[:, :], T.count[:, 0:1], None, ALU.mult)
            v.tensor_scalar(spread[:, 1, :], T.ident[:, :], T.count[:, 0:1], None, ALU.mult)
            v.drain()
            v.sem_inc(packed_made, 1)
            v.sem_inc(ready, 1)
            v.wait_ge(done, 3)
            v.tensor_copy(ends_row[:, :, :], T.psum[:, 4, 0:2 * P])
            v.tensor_scalar(lane0[:, :], lane_f[:, :], -float(S.N), None, ALU.add)
            v.drain()
            v.tensor_scalar(share_i[:, :], ends_row[:, 0, P - 1:P], float(P - 1), None, ALU.add)
            v.drain()
            v.tensor_scalar(share_i[:, :], share_i[:, :], P.bit_length() - 1, None, ALU.logical_shift_right)
            v.drain()
            v.tensor_copy(share[:, :], share_i[:, :])
            v.drain()
            first, old, skip, new_count = (deal[:, k:k + 1] for k in range(4))
            held_by = [deal[:, 4 + k:5 + k] for k in range(PARTS)]
            short, odd = deal[:, 8:9], deal[:, 9:10]
            v.tensor_tensor(first, lane0[:, :], share[:, :], ALU.mult)
            v.drain()
            v.tensor_scalar(pick[:, :], ends_row[:, 0, :], first, None, ALU.is_le)
            v.tensor_tensor(new_count, ends_row[:, 0, P - 1:P], first, ALU.subtract)
            v.drain()
            v.tensor_reduce(old, pick[:, :], AX.X, ALU.add)
            v.tensor_scalar(new_count, new_count, 0.0, share[:, 0:1], ALU.max, ALU.min)
            v.drain()
            v.tensor_tensor(pick[:, :], pick[:, :], ends_row[:, 1, :], ALU.mult)
            v.drain()
            v.tensor_reduce(skip, pick[:, :], AX.X, ALU.add)
            v.drain()
            v.tensor_tensor(skip, first, skip, ALU.subtract)
            for k in range(PARTS):
                v.tensor_scalar(odd, old, float(k), None, ALU.add)
                v.drain()
                v.tensor_scalar(pick[:, :], pos_f[:, 0:P], odd, None, ALU.is_equal)
                v.drain()
                v.tensor_tensor(pick[:, :], pick[:, :], ends_row[:, 1, :], ALU.mult)
                v.drain()
                v.tensor_reduce(held_by[k], pick[:, :], AX.X, ALU.add)
                v.drain()
            v.tensor_tensor(held_by[0], held_by[0], skip, ALU.subtract)
            v.drain()
            for k in range(1, PARTS):
                v.tensor_tensor(held_by[k], held_by[k], held_by[k - 1], ALU.add)
                v.drain()
            v.tensor_tensor(short, new_count, held_by[PARTS - 1], ALU.is_gt)
            v.drain()
            v.sem_inc(ready, 1)
            v.wait_ge(done, 4)
            v.tensor_scalar(odd, T.psum[:, 5, 0:1], 0.0, None, ALU.is_equal)
            v.drain()
            for value, kept in [(old, lane0[:, :]), (new_count, T.count[:, :])] + [(t, T.count[:, :]) for t in held_by]:
                v.tensor_tensor(value, value, kept, ALU.subtract)
                v.drain()
                v.scalar_tensor_tensor(out=value, in0=value, scalar=odd, in1=kept, op0=ALU.mult, op1=ALU.add)
            v.tensor_tensor(skip, skip, odd, ALU.mult)
            v.drain()
            v.tensor_copy(T.count[:, :], new_count)
            for k in range(PARTS):
                v.scalar_tensor_tensor(out=begin[:, k:k + 1], in0=old, scalar=float(W), in1=skip if k == 0 else held_by[k - 1],
                                       op0=ALU.mult, op1=ALU.add if k == 0 else ALU.subtract)
                v.drain()
                v.tensor_scalar(begin_i[:, k:k + 1], begin[:, k:k + 1], float(k * W), 3.0, ALU.add, ALU.mult)
            v.drain()
            v.sem_inc(ready, 1)
            v.sem_inc(begins_made, 1)
            v.wait_ge(parts_in, 16 * PARTS)
            for t, k in ((comp_src, 0), (comp_dst, 1), (comp_own, 2)):
                v.tensor_copy(t[:, :], part[0][:, :, k])
            for n in range(1, PARTS):
                v.tensor_scalar(tmp[:, :], pos_f[:, :], held_by[n - 1], None, ALU.is_ge)
                v.drain()
                for t, k in ((comp_src, 0), (comp_dst, 1), (comp_own, 2)):
                    v.copy_predicated(t[:, :], tmp[:, 0:W].bitcast(I32), part[n][:, :, k])
                v.drain()
            v.tensor_scalar(valid[:, :], pos_f[:, :], T.count[:, 0:1], None, ALU.is_lt)
            v.drain()
            for t, comp in ((T.src, comp_src), (T.dst, comp_dst)):
                v.memset(tmp[:, :], float(NONE))
                v.drain()
                v.copy_predicated(tmp[:, 0:W], valid[:, 0:W].bitcast(I32), comp[:, :])
                v.drain()
                v.tensor_tensor(t[:, 0:LW], tmp[:, :], valid[:, :], ALU.mult)
                v.drain()
            v.memset(T.start[:, :], 0.0)
            v.drain()
            v.tensor_tensor(T.start[:, 1:LW], tmp[:, 1:LW], tmp[:, 0:LW - 1], ALU.not_equal)
            v.drain()
            v.tensor_tensor(T.start[:, 0:LW], T.start[:, 0:LW], valid[:, :], ALU.mult)
            v.drain()
            v.tensor_scalar(T.low_start[:, 0:LW], T.start[:, 0:LW], LOW, None, ALU.mult)
            v.tensor_scalar(T.keep[:, :], T.start[:, 0:LW], -1.0, 1.0, ALU.mult, ALU.add)
            v.tensor_scalar(T.low_pad[:, 0:LW], valid[:, :], -LOW, LOW, ALU.mult, ALU.add)
            v.memset(T.own[:, :], 0.0)
            v.drain()
            v.copy_predicated(T.own[:, 0:W], valid[:, 0:W].bitcast(I32), comp_own[:, :])
            v.drain()
            v.scalar_tensor_tensor(out=T.low_own[:, :], in0=T.own[:, :], scalar=0.0, in1=valid[:, :],
                                   op0=ALU.is_equal, op1=ALU.mult)
            v.drain()
            v.tensor_scalar(T.low_own[:, :], T.low_own[:, :], LOW, None, ALU.mult)
            v.drain()
            v.tensor_tensor(T.low_own1[:, 0:LW], T.low_own[:, :], T.low_pad[:, 0:LW], ALU.add)
            v.tensor_scalar(is_head[:, :], tmp[:, :], tmp[:, 0:1], None, ALU.is_equal)
            v.drain()
            v.tensor_tensor(T.head_end[:, :], is_head[:, :], T.start[:, 1:LW + 1], ALU.mult)
            v.drain()
            v.tensor_reduce(T.has_head[:, :], T.head_end[:, :], AX.X, ALU.add)
            v.tensor_tensor(out_row_f[:, :], tmp[:, :], spare_f[:, :], ALU.subtract)
            v.drain()
            v.tensor_tensor(out_row_f[:, :], out_row_f[:, :], T.start[:, 1:LW + 1], ALU.mult)
            v.drain()
            v.tensor_tensor(T.out_row[:, :], out_row_f[:, :], spare_f[:, :], ALU.add)
            v.tensor_tensor(out_row_f[:, :], out_row_f[:, :], spare_f[:, :], ALU.add)
            v.drain()
            v.tensor_scalar(is_head[:, :], out_row_f[:, :], head_lane[:, 0:1], None, ALU.subtract)
            v.drain()
            v.tensor_tensor(is_head[:, :], is_head[:, :], T.head_end[:, :], ALU.mult)
            v.drain()
            v.tensor_tensor(T.out_row1[:, :], out_row_f[:, :], is_head[:, :], ALU.subtract)
            v.tensor_tensor(T.own_start[:, :], T.own[:, :], T.start[:, 0:LW], ALU.mult)
            v.tensor_tensor(valid[:, 0:LW - 1], valid[:, 0:LW - 1], valid[:, 1:LW], ALU.subtract)
            v.drain()
            v.tensor_tensor(valid[:, :], valid[:, :], tmp[:, :], ALU.mult)
            v.tensor_scalar(empty[:, :], T.count[:, :], 0.0, None, ALU.is_equal)
            v.drain()
            v.tensor_reduce(T.cross.keys[:, 0:1], valid[:, :], AX.X, ALU.add)
            v.drain()
            v.scalar_tensor_tensor(out=T.cross.keys[:, 0:1], in0=empty[:, :], scalar=float(NONE),
                                   in1=T.cross.keys[:, 0:1], op0=ALU.mult, op1=ALU.add)
            v.tensor_copy(T.cross.keys[:, 1:2], tmp[:, 0:1])
            v.drain()
            v.wait_ge(done, 5)
            v.tensor_reduce(most[:, 0:1], T.psum[0:1, 0, 0:P], AX.X, ALU.max)
            v.drain()
            v.tensor_scalar(begun[:, :], pos_f[0:1, 0:LW // EDGE_COLS], float(EDGE_COLS), most[:, 0:1], ALU.mult, ALU.is_lt)
            v.drain()
            v.tensor_reduce(most[:, :], begun[:, :], AX.X, ALU.add)
            v.drain()
            v.tensor_scalar(T.trips[:, :], most[:, :], 2.0, None, ALU.max)
            v.drain()
            T.cross.keys_dve(v, T.psum, ready, done, 6)
            v.tensor_scalar(linked[:, :], T.psum[:, 0, 0:P], T.cross.keys[:, 1:2], None, ALU.is_equal)
            v.drain()
            v.tensor_tensor(linked[:, :], linked[:, :], rank_mask[:, :], ALU.mult)
            v.drain()
            v.tensor_reduce(link[:, :], linked[:, :], AX.X, ALU.add)
            v.drain()
            v.tensor_scalar(link[:, :], link[:, :], 0.0, None, ALU.is_equal)
            v.drain()
            v.tensor_tensor(T.own_start[:, 0:1], T.own[:, 0:1], link[:, :], ALU.mult)
            v.tensor_tensor(rank_mask[:, :], rank_mask[:, :], T.cross.same_tt[:, :], ALU.mult)
            v.drain()
            v.tensor_reduce(tail_first[:, :], rank_mask[:, :], AX.X, ALU.add)
            v.drain()
            v.tensor_scalar(tail_first[:, :], tail_first[:, :], 0.0, None, ALU.is_equal)
            v.drain()
            v.tensor_tensor(empty[:, :], tail_first[:, :], empty[:, :], ALU.is_gt)
            v.drain()
            v.tensor_scalar(tail_first[:, :], T.cross.keys[:, 0:1], lane_f[:, 0:1], None, ALU.subtract)
            v.drain()
            v.tensor_tensor(tail_first[:, :], tail_first[:, :], empty[:, :], ALU.mult)
            v.drain()
            v.tensor_tensor(T.tail_row[:, :], tail_first[:, :], lane_f[:, :], ALU.add)
            v.tensor_reduce(link[:, :], T.cross.same_th[:, :], AX.X, ALU.add)
            v.drain()
            v.tensor_scalar(link[:, :], link[:, :], 0.0, None, ALU.is_equal)
            v.drain()
            v.tensor_tensor(tail_first[:, :], tail_first[:, :], link[:, :], ALU.mult)
            v.drain()
            v.tensor_tensor(T.last_row[:, 0:1], tail_first[:, :], lane_f[:, :], ALU.add)
            v.tensor_scalar(lane_f[:, :], lane_f[:, :], float(P), None, ALU.add)
            v.drain()
            v.tensor_tensor(link[:, :], T.cross.keys[:, 1:2], lane_f[:, :], ALU.subtract)
            v.drain()
            v.tensor_tensor(link[:, :], link[:, :], T.has_head[:, :], ALU.mult)
            v.drain()
            v.tensor_tensor(T.last_row[:, 1:2], link[:, :], lane_f[:, :], ALU.add)

            v.wait_ge(weights_loaded, 96)
            for k in range(2):
                v.wait_ge(att_loaded, 16 * (k + 1))
                for c in range(KC):
                    v.tensor_tensor(prod[:, :], w0[:, c, :], att_b[:, :], ALU.mult)
                    v.drain()
                    v.tensor_reduce(T.r0[:, c, S.IN + k * H0:S.IN + (k + 1) * H0],
                                    prod[:, :].rearrange("p (h c) -> p h c", h=H0), AX.X, ALU.add)
                    v.drain()
                v.sem_inc(att_used, 1)
            for c in range(KC):
                v.tensor_reduce(T.r0[:, c, 0:S.IN], w0[:, c, :].rearrange("p (h c) -> p c h", h=H0), AX.X, ALU.add)
            v.drain()
            v.tensor_scalar(T.r0[:, :, 0:S.IN], T.r0[:, :, 0:S.IN], 1.0 / H0, None, ALU.mult)
            v.tensor_copy(T.v_parts[:, :, 0:2 * H0], T.r0[:, :, S.IN:S.IN + 2 * H0])
            v.drain()
            v.tensor_tensor(T.v_parts[:, :, 2 * H0:4 * H0], T.r0[:, :, S.IN:S.IN + 2 * H0],
                            T.v_parts[:, :, 0:2 * H0].bitcast(F32), ALU.subtract)
            v.tensor_copy(T.w_high[:, :, :], w0[:, :, :])
            v.drain()
            v.tensor_tensor(T.w_low[:, :, :], w0[:, :, :], T.w_high[:, :, :].bitcast(F32), ALU.subtract)
            for k in range(2):
                v.wait_ge(att_loaded, 16 * (k + 3))
                for c in range(KC):
                    m = P if c < KC - 1 else S.CON - P
                    v.tensor_tensor(prod[0:m, 0:S.IN], T.r1[0:m, c, 0:S.IN], att_b[0:m, 0:S.IN], ALU.mult)
                    v.drain()
                    v.tensor_reduce(T.r1[0:m, c, S.IN + k * S.H1:S.IN + (k + 1) * S.H1],
                                    prod[0:m, 0:S.IN].rearrange("p (h c) -> p h c", h=S.H1), AX.X, ALU.add)
                    v.drain()
                v.sem_inc(att_used, 1)
            v.drain()


class Cross:

    def __init__(s, nc, ctx, name, heads, keyed=None):
        s.nc, s.H = nc, heads

        def sb(n, sh, d=F32):
            return ctx.enter_context(nc.sbuf_tensor(f"{name}_{n}", sh, d))
        if keyed:
            s.same_tt, s.same_ht, s.same_th = keyed.same_tt, keyed.same_ht, keyed.same_th
        else:
            s.keys = sb("keys", [P, 2])
            s.head = sb("head_key", [P, 1])
            s.same_tt = sb("same_tt", [P, P])
            s.same_ht = sb("same_ht", [P, P])
            s.same_th = sb("same_th", [P, P])
        s.vals = sb("vals", [P, 2, heads])
        s.total = sb("total", [P, heads])
        s.before = sb("before", [P, heads])
        s.masked = sb("masked", [P, heads, P])
        s.part = sb("part", [P, heads])
        s.pen = sb("pen", [P, P])

    def keys_pe(s, psum, ident, ready, done, n):
        nc = s.nc
        nc.tensor.wait_ge(ready, n)
        nc.tensor.matmul(psum[:, 0, 0:P], s.keys[:, 0:1].broadcast_to([P, P]), ident[:, :], start=True, stop=True)
        nc.tensor.matmul(psum[:, 1, 0:P], s.head[:, :].broadcast_to([P, P]), ident[:, :],
                         start=True, stop=True).then_inc(done, 1)

    def keys_dve(s, v, psum, ready, done, n):
        v.tensor_tensor(s.head[:, :], s.keys[:, 0:1], s.keys[:, 1:2], ALU.is_equal)
        v.drain()
        v.scalar_tensor_tensor(out=s.head[:, :], in0=s.head[:, :], scalar=4.0 * NONE, in1=s.keys[:, 1:2],
                               op0=ALU.mult, op1=ALU.add)
        v.drain()
        v.sem_inc(ready, 1)
        v.wait_ge(done, n)
        v.tensor_scalar(s.same_tt[:, :], psum[:, 0, 0:P], s.keys[:, 0:1], None, ALU.is_equal)
        v.tensor_scalar(s.same_ht[:, :], psum[:, 0, 0:P], s.head[:, 0:1], None, ALU.is_equal)
        v.tensor_scalar(s.same_th[:, :], psum[:, 1, 0:P], s.keys[:, 0:1], None, ALU.is_equal)
        v.drain()

    def scans(s, v, op0, op1, left, values, fwd, bwd, low_start, n, begin, end):
        for h in range(s.H):
            v.tensor_tensor_scan(fwd[:, 0:n, h], left, values[h], begin(h), op0, op1)
        v.drain()
        for h in range(s.H):
            v.tensor_tensor_scan(bwd[:, 0:n, h][:, ::-1], low_start[:, 1:n + 1][:, ::-1], fwd[:, 0:n, h][:, ::-1],
                                 end(h), ALU.add, ALU.max)
        v.drain()

    def sums_pe(s, psum, ready, done, n):
        nc = s.nc
        nc.tensor.wait_ge(ready, n)
        nc.tensor.matmul(psum[:, 2, 0:s.H], s.same_tt[:, :], s.vals[:, 0, :], start=True, stop=False)
        nc.tensor.matmul(psum[:, 2, 0:s.H], s.same_ht[:, :], s.vals[:, 1, :], start=False, stop=True)
        nc.tensor.matmul(psum[:, 3, 0:s.H], s.same_th[:, :], s.vals[:, 0, :], start=True, stop=True).then_inc(done, 1)

    def sums_dve(s, v, psum, vals, fwd, bwd, keep, low_start, n, ready, done, k, values=None):
        vv = [values[:, 0:n] if values is not None else vals[:, 0:n, h] for h in range(s.H)]
        s.scans(v, ALU.mult, ALU.add, keep[:, 0:n], vv, fwd, bwd, low_start, n, lambda h: 0.0, lambda h: LOW)
        v.tensor_copy(s.vals[:, 0, :], fwd[:, n - 1, :])
        v.tensor_copy(s.vals[:, 1, :], bwd[:, 0, :])
        v.drain()
        v.sem_inc(ready, 1)
        v.wait_ge(done, k)
        v.tensor_copy(s.total[:, :], psum[:, 2, 0:s.H])
        v.tensor_copy(s.before[:, :], psum[:, 3, 0:s.H])
        v.drain()
        s.scans(v, ALU.mult, ALU.add, keep[:, 0:n], vv, fwd, bwd, low_start, n,
                lambda h: s.before[:, h:h + 1], lambda h: s.total[:, h:h + 1])

    def maxima_pe(s, psum, ident, ready, done, n):
        nc = s.nc
        nc.tensor.wait_ge(ready, n)
        for k in range(2):
            for h in range(s.H):
                at = psum[:, 2 * k + h // 4, (h % 4) * P:(h % 4 + 1) * P]
                mm = nc.tensor.matmul(at, s.vals[:, k, h:h + 1].broadcast_to([P, P]), ident[:, :],
                                      start=True, stop=True)
        mm.then_inc(done, 1)

    def maxima_dve(s, v, psum, vals, fwd, bwd, low_start, n, ready, done, k):
        vv = [vals[:, 0:n, h] for h in range(s.H)]
        s.scans(v, ALU.add, ALU.max, low_start[:, 0:n], vv, fwd, bwd, low_start, n, lambda h: LOW, lambda h: LOW)
        v.tensor_copy(s.vals[:, 0, :], fwd[:, n - 1, :])
        v.tensor_copy(s.vals[:, 1, :], bwd[:, 0, :])
        v.drain()
        s.join_maxima(v, psum, ready, done, k)
        s.scans(v, ALU.add, ALU.max, low_start[:, 0:n], vv, fwd, bwd, low_start, n,
                lambda h: s.before[:, h:h + 1], lambda h: s.total[:, h:h + 1])

    def join_maxima(s, v, psum, ready, done, k):
        v.sem_inc(ready, 1)
        v.wait_ge(done, k)
        for out, mask, bank in ((s.total, s.same_tt, 0), (s.part, s.same_th, 2), (s.before, s.same_ht, 0)):
            rows = psum[:, bank:bank + s.H // 4, :].rearrange("p b (h q) -> p (b h) q", q=P)
            v.tensor_scalar(s.pen[:, :], mask[:, :], -LOW, LOW, ALU.mult, ALU.add)
            v.drain()
            v.tensor_tensor(s.masked[:, :, :], rows,
                            s.pen[:, :].rearrange("p (o q) -> p o q", o=1).broadcast_to([P, s.H, P]), ALU.add)
            v.drain()
            v.tensor_reduce(out[:, :], s.masked[:, :, :], AX.X, ALU.max)
            v.drain()
        v.tensor_tensor(s.total[:, :], s.total[:, :], s.part[:, :], ALU.max)
        v.drain()


def after(eng, sem, i, per_step, offset, mark=None):
    if isinstance(i, int):
        if per_step * i + offset > 0:
            eng.wait_ge(sem, per_step * i + offset)
    elif mark is None:
        eng.wait_ge(sem, per_step * i + offset)
    else:
        held(eng, sem, per_step * i + offset, mark)


def node_pass(nc, S, T, kind, x, feat=None, logits=None, base=None):
    N, KC, IN, B = S.N, S.KC, S.IN, BATCH
    main, full, pre = kind == "main0", kind == "full1", kind == "logits0"
    AHEAD = 2 if pre else 1
    if full:
        R, OUT, lo = T.r1, IN + 2 * S.H1, 0
    elif main:
        R, OUT, lo = T.r0, IN, 0
    else:
        R, OUT, lo = None, 4 * S.H0, 0
        L = 2 * S.H0
    rows = B * P
    steps = N // rows
    assert steps % SLOTS == 0 and 0 < N - steps * rows <= P, "one last tile covers the rest"
    trips = steps // SLOTS
    I = SLOTS * B
    end = I * trips
    with ExitStack() as ctx:
        def sb(n, s, d=F32):
            return ctx.enter_context(nc.sbuf_tensor(f"{kind}_{n}", s, d))

        def sem(n):
            return ctx.enter_context(nc.semaphore(f"{kind}_{n}"))
        xt = sb("x", [P, I, IN])
        ht = sb("h", [P, I, IN])
        if not pre:
            bt = sb("base", [P, I, IN])
        if not main:
            ot = sb("out", [P, I, L if pre else OUT])
        hT = sb("hT", [P, SLOTS, KC, P], F32R if pre else F32)
        if pre:
            low = sb("low", [P, SLOTS, KC, P], F32R)
        stats = sb("stats", [P, SLOTS, B, 6])
        mv = sb("mv", [P, SLOTS, B, 2])
        std = sb("std", [P, SLOTS, B])
        norm_by = sb("norm_by", [P, SLOTS, 2, B])
        zrow = sb("zrow", [P, IN])
        x_in = [sem(f"x_in{u}") for u in range(SLOTS)]
        moments = sem("moments")
        rooted = sem("rooted")
        scaled = sem("scaled")
        normed = sem("normed")
        based = sem("based")
        turned = sem("turned")
        copied = sem("copied")
        lowered = sem("lowered") if pre else copied
        multiplied = sem("multiplied")
        evacuated = sem("evacuated")
        f_out = sem("f_out")
        feat_st = [sem(f"feat_stored{u}") for u in range(SLOTS)]
        res_st = [sem(f"result_stored{u}") for u in range(SLOTS)]
        zeroed = sem("zeroed")
        spare_st = sem("spare_stored")
        mark = {e: sem(f"mark_{e}") for e in ("sp", "act", "dve", "pool")}
        block = ctx.enter_context(nc.Block())
        GB = T.psum.shape[1] - SLOTS
        assert I % GB == 0

        def bank(n):
            return T.psum[:, n % GB, 0:OUT]

        def turn_bank(n):
            return T.psum[:, GB + n % SLOTS, 0:KC * P]

        def view(dram, s):
            return dram[bass.ds(s * rows, rows), :].rearrange("(p t) c -> p t c", t=B)

        def tile_rows(dram):
            return dram[N - P:N, :]

        def slot(u):
            return slice((u % SLOTS) * B, (u % SLOTS + 1) * B)

        def trip_loop(eng, body):
            for u in range(SLOTS):
                body(0, u)
            with eng.Fori(1, trips - 1) as i:
                for u in range(SLOTS):
                    body(i, u)
            for u in range(SLOTS):
                body(trips - 1, u)

        def behind(i, u, t, do):
            n = B * u + t - LAG
            if n >= 0:
                do(i, n // B, n % B)
            elif not (isinstance(i, int) and i == 0):
                do(i - 1, (n + I) // B, (n + I) % B)

        def inside(i, u):
            return not isinstance(i, int) or SLOTS * i + u < steps

        @block.sync
        def _(sp):
            if base is not None:
                sp.wait_ge(zeroed, 1)
                for k in range(SPARE // P):
                    sp.dma_start(base[N + k * P:N + (k + 1) * P, :], zrow[:, :]).then_inc(spare_st, 16)

            def load(i, u):
                sp.dma_start(xt[:, slot(u), :], view(x, SLOTS * i + u)).then_inc(x_in[u % SLOTS], 16)

            def store_results(i, u):
                if full:
                    after(sp, f_out, i, I, B * (u + 1), mark["sp"])
                    sp.dma_start(view(feat, SLOTS * i + u), ot[:, slot(u), :]).then_inc(feat_st[u % SLOTS], 16)
                after(sp, evacuated, i, I, B * (u + 1), mark["sp"])
                if base is not None:
                    sp.dma_start(view(base[0:N, :], SLOTS * i + u), bt[:, slot(u), :]).then_inc(res_st[u % SLOTS], 16)
                else:
                    sp.dma_start(view(logits, SLOTS * i + u), ot[:, slot(u), :]).then_inc(res_st[u % SLOTS], 16)

            def body(i, u):
                after(sp, normed, i, I, B * (u + 1), mark["sp"])
                if main:
                    sp.dma_start(view(feat, SLOTS * i + u), ht[:, slot(u), :]).then_inc(feat_st[u], 16)
                if inside(i, u + SLOTS):
                    if base is not None:
                        after(sp, based, i, SLOTS, u + 1, mark["sp"])
                    load(i + 1, u)
                if not (isinstance(i, int) and i == 0 and u == 0):
                    store_results(i, u - 1) if u else store_results(i - 1, SLOTS - 1)

            for u in range(SLOTS):
                load(0, u)
            trip_loop(sp, body)
            store_results(trips - 1, SLOTS - 1)
            if base is not None:
                sp.wait_ge(based, steps)
            sp.dma_start(xt[:, 0, :], tile_rows(x)).then_inc(x_in[0], 16)
            for u in range(SLOTS):
                sp.wait_ge(res_st[u], 16 * trips)
                if feat is not None:
                    sp.wait_ge(feat_st[u], 16 * trips)
            sp.wait_ge(evacuated, end + 1)
            if main:
                sp.dma_start(tile_rows(feat), ht[:, 0, :]).then_inc(feat_st[0], 16)
            if full:
                sp.wait_ge(f_out, end + 1)
                sp.dma_start(tile_rows(feat), ot[:, 0, :]).then_inc(feat_st[0], 16)
            if base is not None:
                sp.dma_start(tile_rows(base), bt[:, 0, :]).then_inc(res_st[0], 16)
                sp.wait_ge(spare_st, 16 * (SPARE // P))
            else:
                sp.dma_start(tile_rows(logits), ot[:, 0, :]).then_inc(res_st[0], 16)
            sp.wait_ge(res_st[0], 16 * (trips + 1))
            if feat is not None:
                sp.wait_ge(feat_st[0], 16 * (trips + 1))

        if full:
            @block.gpsimd
            def _(pool):
                def body(i, u):
                    after(pool, normed, i, I, B * (u + 1), mark["pool"])
                    after(pool, res_st[u], i, 16, 0, mark["pool"])
                    pool.tensor_tensor(bt[:, slot(u), :], xt[:, slot(u), :], ht[:, slot(u), :],
                                       ALU.add).then_inc(based, 1)
                trip_loop(pool, body)
                pool.wait_ge(normed, end + 1)
                pool.wait_ge(res_st[0], 16 * trips)
                pool.tensor_tensor(bt[:, 0, :], xt[:, 0, :], ht[:, 0, :], ALU.add).then_inc(based, 1)

        if main:
            @block.gpsimd
            def _(pool):
                T.score_edges(pool)

        @block.scalar
        def _(act):
            def root(i, u):
                if not main:
                    after(act, moments, i, SLOTS, u + 1, mark["act"])
                    act.activation(std[:, u % SLOTS, :], mv[:, u % SLOTS, :, 1], ACT.Sqrt,
                                   bias=T.eps[:, 0:1]).then_inc(rooted, 1)

            def norm(i, u, t):
                if t == 0:
                    after(act, scaled, i, SLOTS, u + 1, mark["act"])
                    if main:
                        after(act, feat_st[u % SLOTS], i + u // SLOTS, 16, 0, mark["act"])
                    if full:
                        after(act, based, i, SLOTS, u + 1 - SLOTS, mark["act"])
                k = (u % SLOTS) * B + t
                by = norm_by[:, u % SLOTS, :, t]
                act.activation(ht[:, k, :], xt[:, k, :], ACT.Relu, bias=by[:, 1:2],
                               scale=by[:, 0:1]).then_inc(normed, 1)

            def copy_turned(i, u, t):
                n = B * u + t
                after(act, turned, i, I, n + 1)
                after(act, multiplied, i, I, n + 1 - SLOTS)
                act.activation(hT[:, n % SLOTS, :, :], turn_bank(n), ACT.Copy).then_inc(copied, 1)

            def take_f(i, u, t):
                n = B * u + t
                after(act, multiplied, i, I, n + 1, mark["act"])
                if t == 0:
                    after(act, feat_st[u], i, 16, 0, mark["act"])
                act.activation(ot[:, n, :], bank(n), ACT.Copy).then_inc(f_out, 1)

            def body(i, u):
                for t in range(B):
                    copy_turned(i, u, t)
                    if full:
                        behind(i, u, t, take_f)
                    if full and t == B - 1 and inside(i, u + 2):
                        root(i, u + 2)
                    if inside(i, u + 1):
                        norm(i, u + 1, t)
                    if not full and t == B - 2 and inside(i, u + 2):
                        root(i, u + 2)

            root(0, 0)
            for t in range(B):
                norm(0, 0, t)
            root(0, 1)
            trip_loop(act, body)
            for n in range(LAG if full else 0):
                behind(trips, 0, n, take_f)
            if not main:
                act.wait_ge(moments, steps + 1)
                act.activation(std[:, 0, 0:1], mv[:, 0, 0:1, 1], ACT.Sqrt, bias=T.eps[:, 0:1]).then_inc(rooted, 1)
            act.wait_ge(scaled, steps + 1)
            if main:
                act.wait_ge(feat_st[0], 16 * trips)
                act.wait_ge(x_in[0], 16 * (trips + 1))
            act.activation(ht[:, 0, :], xt[:, 0, :], ACT.Relu, bias=norm_by[:, 0, 1, 0:1],
                           scale=norm_by[:, 0, 0, 0:1]).then_inc(normed, 1)
            act.wait_ge(turned, end + 1)
            act.activation(hT[:, 0, :, :], turn_bank(0), ACT.Copy).then_inc(copied, 1)
            if full:
                act.wait_ge(multiplied, end + 1)
                act.wait_ge(feat_st[0], 16 * trips)
                act.activation(ot[:, 0, :], bank(0), ACT.Copy).then_inc(f_out, 1)

        @block.tensor
        def _(te):
            def products(n):
                if pre:
                    for k in range(KC):
                        nc.tensor.matmul(bank(n), hT[:, n % SLOTS, k, :], T.v_parts[:, k, :],
                                         start=k == 0, stop=False)
                    for k in range(KC):
                        mm = nc.tensor.matmul(bank(n)[:, 0:L], low[:, n % SLOTS, k, :], T.v_parts[:, k, 0:L],
                                              start=False, stop=k == KC - 1)
                else:
                    for k in range(KC):
                        mm = nc.tensor.matmul(bank(n), hT[:, n % SLOTS, k, :], R[:, k, lo:lo + OUT],
                                              start=k == 0, stop=k == KC - 1)
                mm.then_inc(multiplied, 1)

            def turn(i, n):
                after(te, normed, i, I, n + 1)
                after(te, lowered, i, I, n + 1 - SLOTS)
                for k in range(KC):
                    mm = nc.tensor.transpose(turn_bank(n)[:, k * P:(k + 1) * P],
                                             ht[:, n % I, k * P:(k + 1) * P], T.ident[:, :])
                mm.then_inc(turned, 1)

            def multiply(i, n):
                after(te, lowered, i, I, n + 1)
                after(te, evacuated, i, I, n + 1 - GB)
                products(n)

            def body(i, u):
                for t in range(B):
                    n = B * u + t
                    if not (isinstance(i, int) and I * i + n + AHEAD >= end):
                        turn(i, n + AHEAD)
                    multiply(i, n)
            for n in range(AHEAD):
                turn(0, n)
            trip_loop(te, body)
            te.wait_ge(normed, end + 1)
            for k in range(KC):
                mm = nc.tensor.transpose(turn_bank(0)[:, k * P:(k + 1) * P], ht[:, 0, k * P:(k + 1) * P], T.ident[:, :])
            mm.then_inc(turned, 1)
            te.wait_ge(lowered, end + 1)
            te.wait_ge(evacuated, end)
            products(0)

        @block.vector
        def _(v):
            if base is not None:
                v.memset(zrow[:, :], 0.0).then_inc(zeroed, 1)

            def stats_of(i, u, t):
                if t == 0:
                    after(v, x_in[u % SLOTS], i + u // SLOTS, 16, 16, mark["dve"])
                v.bn_stats(stats[:, u % SLOTS, t, :], xt[:, (u % SLOTS) * B + t, :])

            def moments_of(u):
                v.drain()
                for t in range(B):
                    mm = v.bn_aggr(mv[:, u % SLOTS, t, :], stats[:, u % SLOTS, t, :])
                mm.then_inc(moments, 1)

            def scales_of(i, u):
                k = u % SLOTS
                after(v, normed, i, I, B * (u + 1) - I, mark["dve"])
                if main:
                    after(v, x_in[k], i + u // SLOTS, 16, 16, mark["dve"])
                    if isinstance(i, int):
                        at = T.norms[:, :, (SLOTS * i + u) * B:(SLOTS * i + u + 1) * B]
                    else:
                        at = T.norms[:, :, bass.ds((SLOTS * i + u) * B, B)]
                    v.tensor_copy(norm_by[:, k, :, :], at).then_inc(scaled, 1)
                    return
                after(v, rooted, i, SLOTS, u + 1, mark["dve"])
                v.reciprocal(norm_by[:, k, 0, :], std[:, k, :])
                v.drain()
                v.scalar_tensor_tensor(out=norm_by[:, k, 1, :], in0=mv[:, k, :, 0], scalar=-1.0,
                                       in1=norm_by[:, k, 0, :], op0=ALU.mult, op1=ALU.mult).then_inc(scaled, 1)
                if not full:
                    v.drain()
                    if isinstance(i, int):
                        at = T.norms[:, :, (SLOTS * i + u) * B:(SLOTS * i + u + 1) * B]
                    else:
                        at = T.norms[:, :, bass.ds((SLOTS * i + u) * B, B)]
                    v.tensor_copy(at, norm_by[:, k, :, :])

            def bias_of(i, u):
                after(v, res_st[u % SLOTS], i + u // SLOTS, 16, 0, mark["dve"])
                bias = T.bias_b[:, :].rearrange("p (o c) -> p o c", o=1).broadcast_to([P, B, IN])
                v.tensor_tensor(bt[:, slot(u), :], xt[:, slot(u), :], bias, ALU.add).then_inc(based, 1)

            def lower(i, n):
                after(v, copied, i, I, n + 1, mark["dve"])
                v.tensor_tensor(low[:, n % SLOTS, :, :], turn_bank(n).rearrange("p (k q) -> p k q", k=KC),
                                hT[:, n % SLOTS, :, :].bitcast(F32), ALU.subtract).then_inc(lowered, 1)

            def take_logits(n):
                v.tensor_reduce(ot[:, n, :], bank(n).rearrange("p (a l) -> p l a", a=2), AX.X,
                                ALU.add).then_inc(evacuated, 1)

            def evacuate(i, u, t):
                n = B * u + t
                after(v, f_out if full else multiplied, i, I, n + 1, mark["dve"])
                if t == 0 and full:
                    after(v, based, i, SLOTS, u + 1, mark["dve"])
                if t == 0 and pre:
                    after(v, res_st[u], i, 16, 0, mark["dve"])
                if pre:
                    take_logits(n)
                else:
                    v.tensor_tensor(bt[:, n, :], bank(n)[:, 0:IN], bt[:, n, :], ALU.add).then_inc(evacuated, 1)

            def body(i, u):
                if full and inside(i, u + 1) and not (isinstance(i, int) and i == 0 and u == 0):
                    scales_of(i, u + 1)
                for t in range(B):
                    if not full and t == B - 1:
                        if inside(i, u + 2):
                            scales_of(i, u + 2)
                        if main and inside(i, u + 1):
                            bias_of(i, u + 1)
                            v.drain()
                    if pre:
                        lower(i, B * u + t)
                    if main:
                        evacuate(i, u, t)
                    else:
                        behind(i, u, t, evacuate)
                    if not main and inside(i, u + 2):
                        for k in range(2 * t, min(2 * t + 2, B)):
                            stats_of(i, u + 2, k)
                        if 2 * t < B <= 2 * t + 2:
                            moments_of(u + 2)

            if main:
                scales_of(0, 0)
                scales_of(0, 1)
                bias_of(0, 0)
                v.drain()
            else:
                for u in range(2):
                    for t in range(B):
                        stats_of(0, u, t)
                    moments_of(u)
                    scales_of(0, u)
            trip_loop(v, body)
            for n in range(0 if main else LAG):
                behind(trips, 0, n, evacuate)
            v.wait_ge(x_in[0], 16 * (trips + 1))
            v.wait_ge(normed, end)
            if main:
                v.tensor_copy(norm_by[:, 0, :, 0:1], T.norms[:, :, end:end + 1]).then_inc(scaled, 1)
                v.wait_ge(res_st[0], 16 * trips)
                v.tensor_tensor(bt[:, 0, :], xt[:, 0, :], T.bias_b[:, :], ALU.add).then_inc(based, 1)
                v.drain()
            else:
                v.bn_stats(stats[:, 0, 0, :], xt[:, 0, :])
                v.drain()
                v.bn_aggr(mv[:, 0, 0, :], stats[:, 0, 0, :]).then_inc(moments, 1)
                v.wait_ge(rooted, steps + 1)
                v.reciprocal(norm_by[:, 0, 0, 0:1], std[:, 0, 0:1])
                v.drain()
                v.scalar_tensor_tensor(out=norm_by[:, 0, 1, 0:1], in0=mv[:, 0, 0:1, 0], scalar=-1.0,
                                       in1=norm_by[:, 0, 0, 0:1], op0=ALU.mult, op1=ALU.mult).then_inc(scaled, 1)
                if not full:
                    v.drain()
                    v.tensor_copy(T.norms[:, :, end:end + 1], norm_by[:, 0, :, 0:1])
                    v.wait_ge(res_st[0], 16 * trips)
            if pre:
                lower(trips, 0)
            v.wait_ge(f_out if full else multiplied, end + 1)
            if full:
                v.wait_ge(based, steps + 1)
            if pre:
                take_logits(0)
            else:
                v.tensor_tensor(bt[:, 0, :], bank(0)[:, 0:IN], bt[:, 0, :], ALU.add).then_inc(evacuated, 1)


def scorer(nc, ctx, S, T, logits):
    H, LW, G, N = S.H0, S.LW, EDGE_COLS // 2, S.N

    def sb(n, s, d=F32):
        return ctx.enter_context(nc.sbuf_tensor(f"score_{n}", s, d))

    def sem(n):
        return ctx.enter_context(nc.semaphore(f"score_{n}"))
    ids = sb("ids", [P, 2, 2, G], I32)
    at_src = sb("at_src", [P, 2, G, 2 * H])
    at_dst = sb("at_dst", [P, 2, G, 2 * H])
    cleared, listed = sem("cleared"), sem("listed")
    gathered = [sem(f"gathered{b}") for b in range(2)]
    scored = sem("scored")
    mark = sem("mark")

    def run(pool):
        pool.memset(T.score[:, :, :], 0.0).then_inc(cleared, 1)
        pool.memset(T.score_own[:, :, :], 0.0).then_inc(cleared, 1)
        pool.wait_ge(cleared, 2)
        trips = pool.value_load(T.trips[0:1, 0:1], min_val=2, max_val=LW // (2 * G))

        def gather(i, b):
            after(pool, scored, i, 4, 2 * (b - 1), mark)
            for k, t in enumerate((T.src, T.dst)):
                pool.tensor_copy(ids[:, b, k, :], t[:, bass.ds((2 * i + b) * G, G)]).then_inc(listed, 1)
            after(pool, listed, i, 4, 2 * (b + 1), mark)
            for c in range(G):
                for k, t in enumerate((at_src, at_dst)):
                    pool.indirect_dma_start(
                        out=t[:, b, c, :], out_offset=None, in_=logits[:, :],
                        in_offset=bass.IndirectOffsetOnAxis(ap=ids[:, b, k, c:c + 1], axis=0),
                        bounds_check=N - 1, oob_is_err=False).then_inc(gathered[b], 16)

        def score(i, b):
            cols = bass.ds((2 * i + b) * G, G)
            after(pool, gathered[b], i, 32 * G, 32 * G, mark)
            pool.tensor_tensor(T.score[:, cols, :], at_src[:, b, :, 0:H], at_dst[:, b, :, H:2 * H],
                               ALU.add).then_inc(scored, 1)
            pool.tensor_tensor(T.score_own[:, cols, :], at_dst[:, b, :, 0:H], at_dst[:, b, :, H:2 * H],
                               ALU.add).then_inc(scored, 1)

        gather(0, 0)

        def body(i):
            gather(i, 1)
            score(i, 0)
            gather(i + 1, 0)
            score(i, 1)
        looped(pool, trips, body)
        held(pool, scored, 4 * trips, mark)
        held(pool, gathered[0], 32 * G * (trips + 1), mark)
    return run


def softmax(nc, S, T):
    H, LW = S.H0, S.LW
    cross, score, own = T.cross, T.score, T.score_own
    step = EDGE_COLS
    with ExitStack() as ctx:
        fwd = ctx.enter_context(nc.sbuf_tensor("fwd0", [P, LW, H], F32))
        bwd = ctx.enter_context(nc.sbuf_tensor("bwd0", [P, LW, H], F32))
        ready = ctx.enter_context(nc.semaphore("softmax_rows_ready"))
        done = ctx.enter_context(nc.semaphore("softmax_matmuls_done"))
        shifted = ctx.enter_context(nc.semaphore("shifted"))
        exped = ctx.enter_context(nc.semaphore("exped"))
        block = ctx.enter_context(nc.Block())
        few = -(-(S.E - S.N) // (P * step)) * step

        def by_width(eng, run):
            trips = eng.value_load(T.trips[0:1, 0:1], min_val=2, max_val=LW // step)
            with eng.If(trips < few // step + 1):
                run(few)
            with eng.If(trips > few // step):
                run(LW)

        @block.tensor
        def _(te):
            cross.maxima_pe(T.psum, T.ident, ready, done, 1)
            cross.sums_pe(T.psum, ready, done, 2)

        @block.scalar
        def _(act):
            def run(n):
                act.wait_ge(shifted, 1)
                act.activation(score[:, 0:n, :], score[:, 0:n, :], ACT.Exp).then_inc(exped, 1)
                act.activation(own[:, 0:n, :], own[:, 0:n, :], ACT.Exp).then_inc(exped, 1)
            by_width(act, run)

        @block.vector
        def _(v):
            def run(n):
                for t in (score, own):
                    v.scalar_tensor_tensor(out=t[:, 0:n, :], in0=t[:, 0:n, :], scalar=SLOPE, in1=t[:, 0:n, :],
                                           op0=ALU.mult, op1=ALU.max)
                v.drain()
                v.tensor_tensor(score[:, 0:n, :], score[:, 0:n, :], last(T.low_pad[:, 0:n], H), ALU.add)
                v.tensor_tensor(own[:, 0:n, :], own[:, 0:n, :], last(T.low_own[:, 0:n], H), ALU.add)
                v.drain()
                cross.maxima_dve(v, T.psum, score, fwd, bwd, T.low_start, n, ready, done, 1)
                v.tensor_tensor(bwd[:, 0:n, :], bwd[:, 0:n, :], own[:, 0:n, :], ALU.max)
                v.drain()
                v.tensor_tensor(score[:, 0:n, :], score[:, 0:n, :], bwd[:, 0:n, :], ALU.subtract)
                v.tensor_tensor(own[:, 0:n, :], own[:, 0:n, :], bwd[:, 0:n, :], ALU.subtract).then_inc(shifted, 1)
                v.wait_ge(exped, 2)
                cross.sums_dve(v, T.psum, score, fwd, bwd, T.keep, T.low_start, n, ready, done, 2)
                v.tensor_tensor(own[:, 0:n, :], own[:, 0:n, :], last(T.own[:, 0:n], H), ALU.mult)
                v.drain()
                v.tensor_tensor(bwd[:, 0:n, :], bwd[:, 0:n, :], own[:, 0:n, :], ALU.add)
                v.drain()
                v.tensor_scalar(bwd[:, 0:n, :], bwd[:, 0:n, :], 1e-16, None, ALU.add)
                v.drain()
                v.reciprocal(bwd[:, 0:n, :], bwd[:, 0:n, :])
                v.drain()
                v.scalar_tensor_tensor(out=T.alpha[:, 0:n, :], in0=score[:, 0:n, :], scalar=1.0 / H,
                                       in1=bwd[:, 0:n, :], op0=ALU.mult, op1=ALU.mult)
                v.drain()
            by_width(v, run)


class Rows:

    def __init__(s, nc, ctx, S, T, name, K, width, per):
        s.S, s.T, s.K, s.HALF, s.per = S, T, K, K // 2, per

        def sb(n, sh, d=F32):
            return ctx.enter_context(nc.sbuf_tensor(f"{name}_{n}", sh, d))

        def sem(n):
            return ctx.enter_context(nc.semaphore(f"{name}_{n}"))
        s.ids = sb("ids", [P, 2, 2, K // 2], I32)
        s.outs = sb("outs", [P, 2, K // 2], I32)
        s.rows_s = sb("rows_s", [P, K, width])
        s.rows_d = sb("rows_d", [P, K, width])
        s.out = sb("out", [P, K, S.IN])
        s.cleared = sem("cleared")
        s.listed = sem("listed")
        s.out_listed = sem("out_listed")
        s.gathered = [sem(f"gathered{b}") for b in range(2)]
        s.used = sem("used")
        s.summed = sem("summed")
        s.added = [sem(f"added{k}") for k in range(2 * per)]
        s.mark = sem("mark_rows")

    def landed(s, v, i, b, mark):
        after(v, s.gathered[b], i, 16 * s.K, 16 * s.K, mark)

    def run(s, pool, trips, feat, base, out_row):
        T, K, HALF, N = s.T, s.K, s.HALF, s.S.N

        def gather(i, b):
            after(pool, s.used, i, 2 * s.per, s.per * (b - 1), s.mark)
            for k, t in enumerate((T.src, T.dst)):
                pool.tensor_copy(s.ids[:, b, k, :], t[:, bass.ds((2 * i + b) * HALF, HALF)]).then_inc(s.listed, 1)
            after(pool, s.listed, i, 4, 2 * (b + 1), s.mark)
            for c in range(HALF):
                for k, t in enumerate((s.rows_s, s.rows_d)):
                    pool.indirect_dma_start(
                        out=t[:, b * HALF + c, :], out_offset=None, in_=feat[:, :],
                        in_offset=bass.IndirectOffsetOnAxis(ap=s.ids[:, b, k, c:c + 1], axis=0),
                        bounds_check=N - 1, oob_is_err=False).then_inc(s.gathered[b], 16)

        def scatter(i, b):
            for c in range(s.per):
                after(pool, s.added[b * s.per + c], i, 16 * HALF // s.per, 0, s.mark)
            pool.tensor_copy(s.outs[:, b, :], out_row[:, bass.ds((2 * i + b) * HALF, HALF)]).then_inc(s.out_listed, 1)
            after(pool, s.out_listed, i, 2, b + 1, s.mark)
            for c in range(HALF):
                k = b * HALF + c
                if c < s.per:
                    after(pool, s.summed, i, 2 * s.per, s.per * b + c + 1, s.mark)
                pool.indirect_dma_start(
                    out=base[:, :], out_offset=bass.IndirectOffsetOnAxis(ap=s.outs[:, b, c:c + 1], axis=0),
                    in_=s.out[:, k, :], in_offset=None, bounds_check=N + SPARE - 1, oob_is_err=True,
                    compute_op=ALU.add).then_inc(s.added[b * s.per + c % s.per], 16)

        gather(0, 0)

        def body(i):
            gather(i, 1)
            scatter(i, 0)
            gather(i + 1, 0)
            scatter(i, 1)
        looped(pool, trips, body)
        for sem in s.added:
            held(pool, sem, 16 * HALF // s.per * trips, s.mark)
        held(pool, s.gathered[0], 16 * K * (trips + 1), s.mark)

    def add_last(s, pool, base, rows, values, sem):
        return pool.indirect_dma_start(
            out=base[:, :], out_offset=bass.IndirectOffsetOnAxis(ap=rows, axis=0), in_=values, in_offset=None,
            bounds_check=s.S.N + SPARE - 1, oob_is_err=True, compute_op=ALU.add).then_inc(sem, 16)


def edge_pass0(nc, S, T, feat, base):
    H, K, HALF, IN, KC = S.H0, EDGE_COLS, EDGE_COLS // 2, S.IN, S.KC
    BANKS = H * S.C0 // BANK
    PER = BANK // S.C0
    limit = S.LW // K
    with ExitStack() as ctx:
        def sb(n, s, d=F32):
            return ctx.enter_context(nc.sbuf_tensor(f"e0_{n}", s, d))

        def sem(n):
            return ctx.enter_context(nc.semaphore(f"e0_{n}"))
        R = Rows(nc, ctx, S, T, "e0", K, IN, HALF)
        diff = sb("diff", [P, 2, IN])
        high = sb("high", [P, 2, KC, P], F32R)
        low = sb("low", [P, 2, KC, P], F32R)
        first = sb("first", [P, 2, IN])
        wts = sb("wts", [P, 2, HALF, H + 1])
        tails = sb("tails", [P, IN])
        turned = sem("turned")
        copied = sem("copied")
        lowered = sem("lowered")
        multiplied = sem("multiplied")
        weighted = sem("weighted")
        took = sem("took")
        tails_made = sem("tails_made")
        tails_added = sem("tails_added")
        weights_in = sem("weights_in")
        mark = {e: sem(f"mark_{e}") for e in ("dve", "act", "pe")}
        block = ctx.enter_context(nc.Block())
        cleared = R.cleared

        @block.gpsimd
        def _(pool):
            trips = pool.value_load(T.trips[0:1, 0:1], min_val=2, max_val=limit)
            R.run(pool, trips, feat, base, T.out_row)
            pool.wait_ge(tails_made, 2)
            R.add_last(pool, base, T.tail_row[:, 0:1], tails[:, :], tails_added)
            pool.wait_ge(tails_added, 16)

        @block.tensor
        def _(te):
            te.wait_ge(cleared, 1)
            trips = te.value_load(T.trips[0:1, 0:1], min_val=2, max_val=limit)

            def turn(i, k):
                after(te, R.used, i, K, k + 1)
                after(te, lowered, i, K, k - 1)
                for c in range(KC):
                    mm = nc.tensor.transpose(T.psum[:, 6 + k % 2, c * P:(c + 1) * P],
                                             diff[:, k % 2, c * P:(c + 1) * P], T.ident[:, :])
                mm.then_inc(turned, 1)

            def multiply(i, k, u):
                if u == 0:
                    after(te, lowered, i, K, k + 1)
                after(te, took, i, BANKS * K, BANKS * (k - 1) + u + 1)
                parts = [(high, T.w_high), (high, T.w_low), (low, T.w_high)]
                for c in range(KC):
                    for n, (d, w) in enumerate(parts):
                        mm = nc.tensor.matmul(T.psum[:, u, :], d[:, k % 2, c, :], w[:, c, u * BANK:(u + 1) * BANK],
                                              start=c == 0 and n == 0, stop=c == KC - 1 and n == 2)
                mm.then_inc(multiplied, 1)

            def body(i):
                for k in range(K):
                    for u in range(BANKS):
                        if u == BANKS // 2:
                            turn(i, k + 1) if k < K - 1 else turn(i + 1, 0)
                        multiply(i, k, u)
            turn(0, 0)
            looped(te, trips, body)
            te.wait_ge(tails_made, 1)
            nc.tensor.matmul(T.psum[:, 5, 0:IN], T.cross.same_tt[:, :], R.out[:, K - 1, :],
                             start=True, stop=True).then_inc(turned, 1)

        @block.scalar
        def _(act):
            act.wait_ge(cleared, 1)
            trips = act.value_load(T.trips[0:1, 0:1], min_val=2, max_val=limit)

            def part(i, k):
                after(act, turned, i, K, k + 1, mark["act"])
                after(act, multiplied, i, BANKS * K, BANKS * (k - 1), mark["act"])
                act.activation(high[:, k % 2, :, :], T.psum[:, 6 + k % 2, 0:KC * P], ACT.Copy).then_inc(copied, 1)

            def body(i):
                for k in range(K):
                    after(act, multiplied, i, BANKS * K, BANKS * k + 1, mark["act"])
                    after(act, weights_in, i, 2, k // HALF + 1, mark["act"])
                    after(act, R.summed, i, K, k - 1, mark["act"])
                    act.activation(first[:, k % 2, :], T.psum[:, 0, 0:S.C0], ACT.Copy,
                                   scale=wts[:, k // HALF, k % HALF, 0:1]).then_inc(weighted, 1)
                    part(i, k + 1) if k < K - 1 else part(i + 1, 0)
            part(0, 0)
            looped(act, trips, body)

        @block.vector
        def _(v):
            v.memset(R.out[:, K - 1, :], 0.0)
            v.drain().then_inc(cleared, 1)
            trips = v.value_load(T.trips[0:1, 0:1], min_val=2, max_val=limit)

            def differ(i, k):
                if k % HALF == 0:
                    R.landed(v, i, k // HALF, mark["dve"])
                after(v, turned, i, K, k - 1, mark["dve"])
                v.tensor_tensor(diff[:, k % 2, :], R.rows_s[:, k, :], R.rows_d[:, k, :],
                                ALU.subtract).then_inc(R.used, 1)

            def lower(i, k):
                after(v, copied, i, K, k + 1, mark["dve"])
                after(v, multiplied, i, BANKS * K, BANKS * (k - 1), mark["dve"])
                v.tensor_tensor(low[:, k % 2, :, :],
                                T.psum[:, 6 + k % 2, 0:KC * P].rearrange("p (c q) -> p c q", c=KC),
                                high[:, k % 2, :, :].bitcast(F32), ALU.subtract).then_inc(lowered, 1)

            def take_weights(i, b):
                after(v, weighted, i, K, HALF * (b + 1) - K, mark["dve"])
                at = bass.ds((2 * i + b) * HALF, HALF)
                v.tensor_copy(wts[:, b, :, 0:H], T.alpha[:, at, :])
                v.tensor_copy(wts[:, b, :, H], T.keep[:, at])
                v.drain().then_inc(weights_in, 1)

            def body(i):
                for k in range(K):
                    if k % HALF == 0:
                        take_weights(i, k // HALF)
                    w = wts[:, k // HALF, k % HALF, :]
                    out = R.out[:, k, :]
                    differ(i, k + 1) if k < K - 1 else differ(i + 1, 0)
                    after(v, R.added[k], i, 16, 0, mark["dve"])
                    after(v, weighted, i, K, k + 1, mark["dve"])
                    v.scalar_tensor_tensor(out=out, in0=R.out[:, (k - 1) % K, :], scalar=w[:, H:H + 1],
                                           in1=first[:, k % 2, :], op0=ALU.mult, op1=ALU.add)
                    for h in range(1, H):
                        if h == 2 * PER:
                            lower(i, k + 1) if k < K - 1 else lower(i + 1, 0)
                        if h % PER == 0:
                            after(v, multiplied, i, BANKS * K, BANKS * k + h // PER + 1, mark["dve"])
                        v.drain()
                        mm = v.scalar_tensor_tensor(
                            out=out, in0=T.psum[:, h // PER, (h % PER) * S.C0:(h % PER + 1) * S.C0],
                            scalar=w[:, h:h + 1], in1=out, op0=ALU.mult, op1=ALU.add)
                        if h % PER == PER - 1:
                            mm.then_inc(took, 1)
                    v.drain().then_inc(R.summed, 1)
            differ(0, 0)
            lower(0, 0)
            looped(v, trips, body)
            v.drain().then_inc(tails_made, 1)
            held(v, turned, K * trips + 2, mark["dve"])
            v.tensor_copy(tails[:, :], T.psum[:, 5, 0:IN]).then_inc(tails_made, 1)


def edge_pass1(nc, S, T, feat, base):
    H, K, IN, D = S.H1, EDGE_COLS, S.IN, S.D1
    HALF = K // 2
    limit = S.LW // K
    WIDE = IN + H
    with ExitStack() as ctx:
        def sb(n, s, d=F32):
            return ctx.enter_context(nc.sbuf_tensor(f"e1_{n}", s, d))

        def sem(n):
            return ctx.enter_context(nc.semaphore(f"e1_{n}"))
        R = Rows(nc, ctx, S, T, "e1", K, IN + 2 * H, 1)
        scaled = sb("scaled", [P, IN, HALF + 1])
        factor = sb("factor", [P, IN, HALF + 1])
        acc = sb("acc", [P, IN, HALF + 1])
        low = sb("low", [P, H, HALF + 1])
        raw = sb("raw", [P, 2, H, HALF])
        biased = sb("biased", [P, 2, H, HALF])
        top = sb("top", [P, H, HALF + 1])
        m = sb("m", [P, H, HALF + 1])
        gain = sb("gain", [P, H, HALF + 1])
        l = sb("l", [P, H, HALF + 1])
        args = sb("args", [P, 3, H, HALF + 1])
        exps = sb("exps", [P, 3, H, HALF + 1])
        own_gain = sb("own_gain", [P, H, HALF])
        inv = sb("inv", [P, H, HALF])
        pick = sb("pick", [P, 2, H, HALF])
        picked = sb("picked", [P, 2, H])
        head_acc = sb("head_acc", [P, IN])
        head_ml = sb("head_ml", [P, 2, H])
        tail_ml = sb("tail_ml", [P, 2, H])
        no_head = sb("no_head", [P, 1])
        top_of = sb("top_of", [P, 2, H])
        scale = sb("scale", [P, 2, H])
        wide = sb("wide", [P, 2, WIDE])
        joint = sb("joint", [P, 2, WIDE])
        last_out = sb("last_out", [P, 2, IN])
        maxed = sem("maxed")
        exped = sem("exped")
        ready = sem("ready")
        done = sem("done")
        heads_back = sem("heads_back")
        lasts_made = sem("lasts_made")
        lasts_added = sem("lasts_added")
        mark = {e: sem(f"mark_{e}") for e in ("dve", "act")}
        block = ctx.enter_context(nc.Block())
        cross = T.cross1

        def heads(ap):
            return ap.rearrange("p (h d) -> p h d", h=H)

        def over_head(ap):
            return ap.rearrange("p h (o c) -> p h o c", o=1).broadcast_to([P, H, D, ap.shape[2]])

        def over_heads(ap):
            return ap.rearrange("p (o c) -> p o c", o=1).broadcast_to([P, H, ap.shape[1]])

        def flat(ap):
            return ap.rearrange("p f c -> p (f c)")

        @block.gpsimd
        def _(pool):
            trips = pool.value_load(T.trips[0:1, 0:1], min_val=2, max_val=limit)
            R.run(pool, trips, feat, base, T.out_row1)
            pool.dma_start(head_acc[:, :], base[S.N + HEADS_AT:S.N + SPARE, :]).then_inc(heads_back, 16)
            pool.wait_ge(lasts_made, 1)
            for k in range(2):
                R.add_last(pool, base, T.last_row[:, k:k + 1], last_out[:, k, :], lasts_added)
            pool.wait_ge(lasts_added, 32)

        @block.scalar
        def _(act):
            act.wait_ge(R.cleared, 1)
            trips = act.value_load(T.trips[0:1, 0:1], min_val=2, max_val=limit)

            def exp(i, b):
                after(act, maxed, i, 2, b + 1, mark["act"])
                act.activation(exps[:, :, :, :], args[:, :, :, :], ACT.Exp).then_inc(exped, 1)
                act.activation(factor[:, :, :].rearrange("p (h d) c -> p h d c", h=H), over_head(args[:, 2, :, :]),
                               ACT.Exp).then_inc(exped, 1)

            def body(i):
                exp(i, 0)
                exp(i, 1)
            looped(act, trips, body)
            held(act, maxed, 2 * trips + 1, mark["act"])
            act.activation(scale[:, :, :], top_of[:, :, :], ACT.Exp).then_inc(exped, 1)

        @block.tensor
        def _(te):
            cross.maxima_pe(T.psum, T.ident, ready, done, 1)
            te.wait_ge(ready, 2)
            nc.tensor.matmul(T.psum[:, 4, 0:WIDE], cross.same_tt[:, :], wide[:, 0, :], start=True, stop=False)
            nc.tensor.matmul(T.psum[:, 4, 0:WIDE], cross.same_ht[:, :], wide[:, 1, :], start=False, stop=True)
            nc.tensor.matmul(T.psum[:, 5, 0:WIDE], cross.same_th[:, :], wide[:, 0, :],
                             start=True, stop=True).then_inc(done, 1)

        @block.vector
        def _(v):
            v.memset(acc[:, :, :], 0.0)
            v.memset(m[:, :, :], LOW)
            v.memset(l[:, :, :], 0.0)
            v.memset(head_ml[:, :, :], 0.0)
            v.memset(args[:, :, :, :], LOW)
            v.memset(low[:, :, :], LOW)
            v.drain().then_inc(R.cleared, 1)
            trips = v.value_load(T.trips[0:1, 0:1], min_val=2, max_val=limit)

            def by_head(ap):
                return ap.rearrange("p c h -> p h c")

            def by_feature(ap):
                return ap.rearrange("p c (h d) -> p h d c", h=H)

            def split(ap):
                return ap.rearrange("p (h d) c -> p h d c", h=H)

            def half(i, b):
                R.landed(v, i, b, mark["dve"])
                cols = bass.ds((2 * i + b) * HALF, HALF)
                rows = slice(b * HALF, (b + 1) * HALF)
                new = slice(1, HALF + 1)
                s_src = by_head(R.rows_s[:, rows, IN:IN + H])
                d_src, d_dst = by_head(R.rows_d[:, rows, IN:IN + H]), by_head(R.rows_d[:, rows, IN + H:IN + 2 * H])
                v.tensor_tensor(raw[:, 0, :, :], s_src, d_dst, ALU.add)
                v.tensor_tensor(raw[:, 1, :, :], d_src, d_dst, ALU.add)
                v.tensor_copy(top[:, :, 0:1], m[:, :, HALF:])
                v.tensor_copy(low[:, :, new], over_heads(T.low_start[:, cols]))
                v.drain()
                v.scalar_tensor_tensor(out=biased[:, :, :, :].rearrange("p a h c -> p (a h c)"),
                                       in0=raw[:, :, :, :].rearrange("p a h c -> p (a h c)"), scalar=SLOPE,
                                       in1=raw[:, :, :, :].rearrange("p a h c -> p (a h c)"),
                                       op0=ALU.mult, op1=ALU.max)
                v.drain()
                v.tensor_tensor(biased[:, 0, :, :], biased[:, 0, :, :], over_heads(T.low_pad[:, cols]), ALU.add)
                v.tensor_tensor(biased[:, 1, :, :], biased[:, 1, :, :], over_heads(T.low_own1[:, cols]), ALU.add)
                v.drain()
                v.tensor_tensor(top[:, :, new], biased[:, 0, :, :], biased[:, 1, :, :], ALU.max)
                v.drain()
                v.tensor_tensor_scan(flat(m[:, :, :]), flat(low[:, :, :]), flat(top[:, :, :]), LOW, ALU.add, ALU.max)
                v.drain()
                for k in range(2):
                    v.tensor_tensor(args[:, k, :, new], biased[:, k, :, :], m[:, :, new], ALU.subtract)
                v.tensor_tensor(args[:, 2, :, new], m[:, :, 0:HALF], m[:, :, new], ALU.subtract)
                v.drain()
                v.tensor_tensor(args[:, 2, :, new], args[:, 2, :, new], low[:, :, new], ALU.add)
                v.drain().then_inc(maxed, 1)
                v.tensor_tensor(split(scaled[:, :, new]), by_feature(R.rows_s[:, rows, 0:IN]),
                                by_feature(R.rows_d[:, rows, 0:IN]), ALU.subtract).then_inc(R.used, 1)
                v.tensor_copy(scaled[:, :, 0:1], acc[:, :, HALF:])
                v.tensor_copy(gain[:, :, 0:1], l[:, :, HALF:])
                after(v, exped, i, 4, 2 * (b + 1), mark["dve"])
                v.tensor_tensor(own_gain[:, :, :], exps[:, 1, :, new], over_heads(T.own_start[:, cols]), ALU.mult)
                v.drain()
                v.tensor_tensor(split(scaled[:, :, new]), split(scaled[:, :, new]), over_head(exps[:, 0, :, new]), ALU.mult)
                v.tensor_tensor(gain[:, :, new], own_gain[:, :, :], exps[:, 0, :, new], ALU.add)
                v.drain()
                v.tensor_tensor_scan(flat(l[:, :, :]), flat(exps[:, 2, :, :]), flat(gain[:, :, :]), 0.0, ALU.mult, ALU.add)
                v.tensor_tensor_scan(flat(acc[:, :, :]), flat(factor[:, :, :]), flat(scaled[:, :, :]), 0.0, ALU.mult, ALU.add)
                v.drain()
                v.tensor_scalar(inv[:, :, :], l[:, :, new], 1e-30, None, ALU.max)
                v.tensor_tensor(pick[:, 0, :, :], m[:, :, new], over_heads(T.head_end[:, cols]), ALU.mult)
                v.tensor_tensor(pick[:, 1, :, :], l[:, :, new], over_heads(T.head_end[:, cols]), ALU.mult)
                v.drain()
                v.reciprocal(inv[:, :, :], inv[:, :, :])
                for k in range(2):
                    v.tensor_reduce(picked[:, k, :], pick[:, k, :, :], AX.X, ALU.add)
                after(v, R.added[b], i, 16 * HALF, 0, mark["dve"])
                v.drain()
                v.tensor_tensor(by_feature(R.out[:, rows, :]), split(acc[:, :, new]), over_head(inv[:, :, :]),
                                ALU.mult).then_inc(R.summed, 1)
                v.tensor_tensor(head_ml[:, :, :], head_ml[:, :, :], picked[:, :, :], ALU.add)

            def body(i):
                half(i, 0)
                half(i, 1)
            looped(v, trips, body)
            v.drain()
            v.tensor_copy(tail_ml[:, 0, :], m[:, :, HALF])
            v.tensor_copy(tail_ml[:, 1, :], l[:, :, HALF])
            v.tensor_scalar(no_head[:, :], T.has_head[:, :], -LOW, LOW, ALU.mult, ALU.add)
            v.drain()
            v.tensor_copy(cross.vals[:, 0, :], tail_ml[:, 0, :])
            v.tensor_scalar(cross.vals[:, 1, :], head_ml[:, 0, :], no_head[:, 0:1], None, ALU.add)
            v.drain()
            cross.join_maxima(v, T.psum, ready, done, 1)
            v.tensor_copy(top_of[:, 0, :], cross.total[:, :])
            v.tensor_tensor(top_of[:, 1, :], cross.before[:, :], cross.vals[:, 1, :], ALU.max)
            v.drain()
            v.tensor_tensor(top_of[:, :, :], cross.vals[:, :, :], top_of[:, :, :], ALU.subtract)
            v.drain().then_inc(maxed, 1)
            held(v, exped, 4 * trips + 1, mark["dve"])
            v.wait_ge(heads_back, 16)
            v.tensor_tensor(heads(head_acc[:, :]), heads(head_acc[:, :]), last(head_ml[:, 1, :], D), ALU.mult)
            v.drain()
            for k, (a, ml) in enumerate(((acc[:, :, HALF], tail_ml), (head_acc[:, :], head_ml))):
                v.tensor_tensor(heads(wide[:, k, 0:IN]), heads(a), last(scale[:, k, :], D), ALU.mult)
                v.tensor_tensor(wide[:, k, IN:WIDE], ml[:, 1, :], scale[:, k, :], ALU.mult)
            v.drain().then_inc(ready, 1)
            v.wait_ge(done, 2)
            v.tensor_copy(joint[:, 0, :], T.psum[:, 4, 0:WIDE])
            v.tensor_tensor(joint[:, 1, :], T.psum[:, 5, 0:WIDE], wide[:, 1, :], ALU.add)
            v.drain()
            v.tensor_scalar(scale[:, :, :], joint[:, :, IN:WIDE], 1e-30, None, ALU.max)
            v.drain()
            v.reciprocal(scale[:, :, :], scale[:, :, :])
            v.drain()
            for k in range(2):
                v.tensor_tensor(heads(last_out[:, k, :]), heads(joint[:, k, 0:IN]), last(scale[:, k, :], D), ALU.mult)
            v.drain().then_inc(lasts_made, 1)


class Tables:
    pass


def program(nc, x, src, dst, W0, att0s, att0d, bias, W1, attn_s, attn_d, pos_s, pos_d, out):
    S = Sizes(x, src, W0, att0s, W1, attn_s, pos_s)
    T = Tables()
    h0 = nc.dram_tensor("h0", (S.N, S.IN), F32, kind="Internal").ap()
    x1 = nc.dram_tensor("x1", (S.N + SPARE, S.IN), F32, kind="Internal").ap()
    f1 = nc.dram_tensor("f1", (S.N, S.IN + 2 * S.H1), F32, kind="Internal").ap()
    lists = nc.dram_tensor("lists", ((P + LIST_PADS) * S.W, 3), F32, kind="Internal").ap()
    logits0 = nc.dram_tensor("logits0", (S.N, 2 * S.H0), F32, kind="Internal").ap()
    with ExitStack() as ctx:
        def sb(n, s, d=F32):
            return ctx.enter_context(nc.sbuf_tensor(n, s, d))
        T.psum = ctx.enter_context(nc.psum_tensor("psum", [P, 8, BANK], F32))
        T.src = sb("list_src", [P, S.LW + EDGE_COLS], I32)
        T.dst = sb("list_dst", [P, S.LW + EDGE_COLS], I32)
        T.start = sb("list_start", [P, S.LW + 1])
        T.low_start = sb("list_low_start", [P, S.LW + EDGE_COLS])
        T.keep = sb("list_keep", [P, S.LW])
        T.low_pad = sb("list_low_pad", [P, S.LW + EDGE_COLS])
        T.own = sb("list_own", [P, S.LW])
        T.own_start = sb("list_own_start", [P, S.LW])
        T.low_own = sb("list_low_own", [P, S.LW])
        T.low_own1 = sb("list_low_own1", [P, S.LW + EDGE_COLS])
        T.head_end = sb("list_head_end", [P, S.LW])
        T.out_row = sb("list_out_row", [P, S.LW], I32)
        T.out_row1 = sb("list_out_row1", [P, S.LW], I32)
        T.tail_row = sb("tail_row", [P, 1], I32)
        T.last_row = sb("last_row", [P, 2], I32)
        T.has_head = sb("has_head", [P, 1])
        T.count = sb("count", [P, 1])
        T.trips = sb("trips", [1, 1], I32)
        T.eps = sb("eps", [P, 1])
        T.ident = sb("ident", [P, P])
        T.bias_b = sb("bias_b", [P, S.IN])
        T.norms = sb("norms", [P, 2, -(-S.N // P)])
        T.w_high = sb("w_high", [P, S.KC, S.H0 * S.C0], F32R)
        T.w_low = sb("w_low", [P, S.KC, S.H0 * S.C0], F32R)
        T.v_parts = sb("v_parts", [P, S.KC, 4 * S.H0], F32R)
        T.r0 = sb("r0", [P, S.KC, S.IN + 2 * S.H0])
        T.r1 = sb("r1", [P, S.KC, S.IN + 2 * S.H1])
        T.cross = Cross(nc, ctx, "cross0", S.H0)
        T.cross1 = Cross(nc, ctx, "cross1", S.H1, T.cross)
        prepare(nc, S, T, lists, src, dst, W0, att0s, att0d, W1, attn_s, attn_d, pos_s, pos_d, bias)
        node_pass(nc, S, T, "logits0", x, logits=logits0)
        with ExitStack() as inner:
            T.alpha = inner.enter_context(nc.sbuf_tensor("alpha", [P, S.LW, S.H0], F32))
            with ExitStack() as scoring:
                T.score = scoring.enter_context(nc.sbuf_tensor("score", [P, S.LW, S.H0], F32))
                T.score_own = scoring.enter_context(nc.sbuf_tensor("score_own", [P, S.LW, S.H0], F32))
                with ExitStack() as c:
                    T.score_edges = scorer(nc, c, S, T, logits0)
                    node_pass(nc, S, T, "main0", x, feat=h0, base=x1)
                softmax(nc, S, T)
            edge_pass0(nc, S, T, h0, x1)
        node_pass(nc, S, T, "full1", x1, feat=f1, base=out)
        edge_pass1(nc, S, T, f1, out)


_INS = ['x', 'src', 'dst', 'L0_gnn_W', 'L0_gnn_att_src', 'L0_gnn_att_dst', 'L0_gnn_bias', 'L1_gnn_W',
        'L1_gnn_attn_src', 'L1_gnn_attn_dst', 'L1_gnn_pos_attn_src', 'L1_gnn_pos_attn_dst']


def kernel(**inputs):
    import numpy as _np
    import concourse.bacc as _bacc
    from concourse import mybir as _mybir
    from concourse.bass_utils import run_bass_kernel_spmd as _run

    nc = _bacc.Bacc("TRN2", target_bir_lowering=False, num_devices=1)
    arrays, args = {}, []
    for name in _INS:
        a = _np.ascontiguousarray(inputs[name])
        arrays[f"in_{name}_dram"] = a
        args.append(nc.dram_tensor(f"in_{name}_dram", a.shape, _mybir.dt.from_np(a.dtype), kind="ExternalInput").ap())
    n, c = inputs['x'].shape
    out = nc.dram_tensor("out_0_dram", (n + SPARE, c), _mybir.dt.float32, kind="ExternalOutput").ap()
    program(nc, *args, out)
    r = _run(nc, [arrays], core_ids=[0])
    return r.results[0]["out_0_dram"][:n]
```

```python
import concourse.bass as bass
from concourse import mybir
from contextlib import ExitStack

F32 = mybir.dt.float32
F32R = mybir.dt.float32r
I32 = mybir.dt.int32
ALU = mybir.AluOpType
ACT = mybir.ActivationFunctionType
AX = mybir.AxisListType

P = 128
EPS = 1e-5
SLOPE = 0.2
NONE = 60000
LOW = -1e30
BANK = 512

EDGE_COLS = 14
HEADS_AT = EDGE_COLS * P
SPARE = HEADS_AT + P
PARTS = 3
LIST_PADS = PARTS + 1
BATCH = 5
LAG = 2
SLOTS = 3


def last(ap, n):
    return ap.rearrange("p (m o) -> p m o", o=1).broadcast_to([ap.shape[0], ap.shape[1], n])


def held(eng, sem, value, mark):
    eng.wait_ge(sem, value)
    eng.sem_inc(mark, 1)


def looped(eng, count, body):
    body(0)
    with eng.Fori(1, count) as i:
        body(i)


class Sizes:
    def __init__(s, x, src, W0, att0, W1, attn1, pos1):
        s.N, s.IN = x.shape
        s.E = src.shape[0]
        s.H0, s.C0 = att0.shape
        _, s.H1, s.D1 = attn1.shape
        s.POS = pos1.shape[2]
        s.CON = s.IN - s.POS
        s.W = -(-s.E // P)
        s.LW = -(-s.W // EDGE_COLS) * EDGE_COLS
        s.KC = s.IN // P


def prepare(nc, S, T, lists, src, dst, W0, att0s, att0d, W1, pos_s, pos_d, bias):
    W, LW, KC, H0, C0 = S.W, S.LW, S.KC, S.H0, S.C0
    full = P - 1
    rest = S.E - full * W
    with ExitStack() as ctx:
        def sb(n, s, d=F32):
            return ctx.enter_context(nc.sbuf_tensor(n, s, d))

        def sem(n):
            return ctx.enter_context(nc.semaphore(n))
        src_i = sb("src_i", [P, W], I32)
        dst_i = sb("dst_i", [P, W], I32)
        src_f = sb("src_f", [P, W])
        dst_f = sb("dst_f", [P, W])
        own = sb("own", [P, W])
        start = sb("start", [P, W])
        low_start = sb("low_start", [P, W + 1])
        keep = sb("keep", [P, W])
        fwd = sb("fwd", [P, W, 1])
        own_count = sb("own_count", [P, W, 1])
        place = sb("place", [P, W])
        shift = [sb(f"shift{i}", [P, W], I32) for i in range(2)]
        moved = sb("moved", [P, W], I32)
        comp_src = sb("comp_src", [P, W])
        comp_dst = sb("comp_dst", [P, W])
        comp_own = sb("comp_own", [P, W])
        ones = sb("ones", [P, W])
        packed = sb("packed", [P, W, 3])
        part = [packed] + [sb(f"part{k}", [P, W, 3]) for k in range(1, PARTS)]
        pads = sb("pads", [LIST_PADS, W * 3])
        upto = sb("upto", [P, P])
        spread = sb("spread", [P, 2, P])
        ones_pp = sb("ones_pp", [P, P])
        ends_row = sb("ends_row", [P, 2, P])
        pick = sb("pick", [P, P])
        share_i = sb("share_i", [P, 1], I32)
        share = sb("share", [P, 1])
        lane0 = sb("lane0", [P, 1])
        begin = sb("begin", [P, PARTS])
        deal = sb("deal", [P, 12])
        begin_i = sb("begin_i", [P, PARTS], I32)
        most = sb("most", [1, 1])
        begun = sb("begun", [1, LW // EDGE_COLS])
        pos_i = sb("pos_i", [P, LW], I32)
        pos_f = sb("pos_f", [P, LW])
        valid = sb("valid", [P, LW])
        spare_i = sb("spare_i", [P, LW], I32)
        spare_f = sb("spare_f", [P, LW])
        lane_i = sb("lane_i", [P, 1], I32)
        lane_f = sb("lane_f", [P, 1])
        head_lane = sb("head_lane", [P, 1])
        empty = sb("empty", [P, 1])
        w0 = sb("w0", [P, KC, H0 * C0])
        out_row_f = sb("out_row_f", [P, LW])
        is_head = sb("is_head", [P, LW])
        linked = sb("linked", [P, P])
        link = sb("link", [P, 1])
        att_b = sb("att_b", [P, H0 * C0])
        prod = sb("prod", [P, H0 * C0])
        tmp = sb("tmp", [P, LW])
        rank_mask = sb("rank_mask", [P, P])
        tail_first = sb("tail_first", [P, 1])
        cross = Cross(nc, ctx, "own", 1)
        loaded = sem("edges_loaded")
        padded = sem("edges_padded")
        weights_loaded = sem("weights_loaded")
        constants = sem("constants")
        upto_set = sem("upto_set")
        att_loaded = sem("att_loaded")
        att_used = sem("att_used")
        ready = sem("rows_ready")
        done = sem("matmuls_done")
        weights_zeroed = sem("weights_zeroed")
        packed_made = sem("packed_made")
        packed_stored = sem("packed_stored")
        begins_made = sem("begins_made")
        parts_in = sem("parts_in")
        block = ctx.enter_context(nc.Block())

        @block.sync
        def _(sp):
            sp.dma_start(w0[:, :, :], W0.rearrange("(k p) n -> p k n", p=P)).then_inc(weights_loaded, 16)
            sp.dma_start(T.bias_b[:, :], bias.partition_broadcast(P)).then_inc(weights_loaded, 16)
            sp.wait_ge(weights_zeroed, 1)
            top = S.CON - P
            sp.dma_start(T.r1[:, 0, 0:S.IN], W1[0:P, :]).then_inc(weights_loaded, 16)
            sp.dma_start(T.r1[0:top, 1, 0:S.IN], W1[P:S.CON, :]).then_inc(weights_loaded, 16)
            for k, pos in enumerate((pos_s, pos_d)):
                c = S.IN + k * S.H1
                sp.dma_start(T.r1[top:P, 1, c:c + S.H1], pos[0].rearrange("h p -> p h"),
                             allow_slow_non_contiguous=True).then_inc(weights_loaded, 16)
            sp.wait_ge(padded, 2)
            for tile, dram in ((src_i, src), (dst_i, dst)):
                rows = dram[0:full * W].rearrange("(p w) -> p w", w=W)
                for a, b in ((0, 112), (112, full)):
                    sp.dma_start(tile[a:b, :], rows[a:b, :]).then_inc(loaded, 16)
                sp.dma_start(tile[full:P, 0:rest],
                             dram[full * W:S.E].rearrange("(o w) -> o w", o=1)).then_inc(loaded, 16)
            sp.wait_ge(packed_made, 1)
            sp.dma_start(lists[0:P * W, :].rearrange("(p w) c -> p (w c)", w=W),
                         packed[:, :, :].rearrange("p w c -> p (w c)")).then_inc(packed_stored, 16)
            sp.dma_start(lists[P * W:(P + LIST_PADS) * W, :].rearrange("(p w) c -> p (w c)", w=W),
                         pads[:, :]).then_inc(packed_stored, 16)
            for k, vec in enumerate((att0s, att0d)):
                if k:
                    sp.wait_ge(att_used, k)
                sp.dma_start(att_b[:, :], vec.partition_broadcast(P)).then_inc(att_loaded, 16)
            sp.wait_ge(att_loaded, 32)
            sp.wait_ge(loaded, 96)
            sp.wait_ge(weights_loaded, 96)

        @block.gpsimd
        def _(pool):
            pool.memset(T.ident[:, :], 0.0).then_inc(constants, 1)
            pool.memset(rank_mask[:, :], 1.0).then_inc(constants, 1)
            pool.wait_ge(constants, 2)
            pool.affine_select(out=T.ident[:, :], in_=T.ident[:, :], compare_op=ALU.not_equal, fill=1.0,
                               base=0, pattern=[[-1, P]], channel_multiplier=1).then_inc(constants, 1)
            pool.affine_select(out=rank_mask[:, :], in_=rank_mask[:, :], compare_op=ALU.is_gt, fill=0.0,
                               base=0, pattern=[[-1, P]], channel_multiplier=1).then_inc(constants, 1)
            pool.iota(pos_i[:, :], [[1, LW]], 0, channel_multiplier=0).then_inc(constants, 1)
            pool.iota(spare_i[:, :], [[0, LW // EDGE_COLS], [P, EDGE_COLS]], S.N, channel_multiplier=1).then_inc(constants, 1)
            pool.iota(lane_i[:, :], [[1, 1]], S.N, channel_multiplier=1).then_inc(constants, 1)
            pool.memset(upto[:, :], 1.0).then_inc(upto_set, 1)
            pool.wait_ge(upto_set, 1)
            pool.affine_select(out=upto[:, :], in_=upto[:, :], compare_op=ALU.is_ge, fill=0.0,
                               base=0, pattern=[[1, P]], channel_multiplier=-1).then_inc(constants, 1)
            pool.wait_ge(packed_stored, 32)
            pool.wait_ge(begins_made, 1)
            for k in range(PARTS):
                pool.indirect_dma_start(
                    out=part[k][:, :, :].rearrange("p w c -> p (w c)"), out_offset=None,
                    in_=lists.rearrange("n c -> (n c)").rearrange("(n o) -> n o", o=1),
                    in_offset=bass.IndirectOffsetOnAxis(ap=begin_i[:, k:k + 1], axis=0),
                    bounds_check=(P + LIST_PADS) * W * 3 - 1, oob_is_err=False).then_inc(parts_in, 16)

        @block.tensor
        def _(te):
            te.wait_ge(constants, 8)
            cross.keys_pe(T.psum, T.ident, ready, done, 1)
            cross.sums_pe(T.psum, ready, done, 2)
            te.wait_ge(ready, 3)
            nc.tensor.matmul(T.psum[:, 4, 0:2 * P], ones_pp[:, :], spread[:, :, :],
                             start=True, stop=True).then_inc(done, 1)
            te.wait_ge(ready, 4)
            nc.tensor.matmul(T.psum[:, 5, 0:1], ones_pp[:, :], deal[:, 8:9], start=True, stop=True).then_inc(done, 1)
            te.wait_ge(ready, 5)
            nc.tensor.transpose(T.psum[0:1, 0, 0:P], T.count[:, :], T.ident[:, :]).then_inc(done, 1)
            T.cross.keys_pe(T.psum, T.ident, ready, done, 6)

        @block.vector
        def _(v):
            v.memset(src_i[:, :], NONE).then_inc(padded, 1)
            v.memset(dst_i[:, :], NONE).then_inc(padded, 1)
            v.memset(T.r1[:, :, :], 0.0).then_inc(weights_zeroed, 1)
            v.memset(T.eps[:, :], EPS)
            v.memset(ones[:, :], 1.0)
            v.memset(ones_pp[:, :], 1.0)
            v.memset(pads[:, :], 0.0)
            v.memset(T.src[:, LW:], 0)
            v.memset(T.dst[:, LW:], 0)
            v.memset(T.low_start[:, LW:], 0.0)
            v.memset(T.low_pad[:, LW:], LOW)
            v.memset(T.low_own1[:, LW:], LOW)
            v.wait_ge(constants, 8)
            v.tensor_copy(pos_f[:, :], pos_i[:, :])
            v.tensor_copy(lane_f[:, :], lane_i[:, :])
            v.tensor_scalar(head_lane[:, :], lane_i[:, :], float(HEADS_AT), None, ALU.add)
            v.tensor_copy(spare_f[:, :], spare_i[:, :])
            v.wait_ge(loaded, 96)
            v.tensor_copy(src_f[:, :], src_i[:, :])
            v.tensor_copy(dst_f[:, :], dst_i[:, :])
            v.drain()
            v.memset(start[:, 0:1], 0.0)
            v.tensor_tensor(start[:, 1:W], dst_f[:, 1:W], dst_f[:, 0:W - 1], ALU.not_equal)
            v.tensor_tensor(own[:, :], src_f[:, :], dst_f[:, :], ALU.is_equal)
            v.memset(low_start[:, W:W + 1], 0.0)
            v.tensor_copy(cross.keys[:, 0:1], dst_f[:, W - 1:W])
            v.tensor_copy(cross.keys[:, 1:2], dst_f[:, 0:1])
            v.drain()
            v.tensor_scalar(low_start[:, 0:W], start[:, :], LOW, None, ALU.mult)
            v.tensor_scalar(keep[:, :], start[:, :], -1.0, 1.0, ALU.mult, ALU.add)
            v.drain()
            cross.keys_dve(v, T.psum, ready, done, 1)
            v.tensor_copy(fwd[:, :, 0], own[:, :])
            v.drain()
            cross.sums_dve(v, T.psum, fwd, fwd, own_count, keep, low_start, W, ready, done, 2, values=own)
            v.tensor_scalar(tmp[:, 0:W], own[:, :], -1.0, 1.0, ALU.mult, ALU.add)
            v.drain()
            v.tensor_tensor_scan(place[:, :], ones[:, :], tmp[:, 0:W], 0.0, ALU.mult, ALU.add)
            v.drain()
            v.tensor_copy(T.count[:, :], place[:, W - 1:W])
            v.drain()
            v.scalar_tensor_tensor(out=place[:, :], in0=pos_f[:, 0:W], scalar=1.0, in1=place[:, :],
                                   op0=ALU.add, op1=ALU.subtract)
            v.drain()
            v.tensor_tensor(shift[0][:, :], place[:, :], tmp[:, 0:W], ALU.mult)
            v.tensor_copy(comp_src[:, :], src_f[:, :])
            v.tensor_copy(comp_dst[:, :], dst_f[:, :])
            v.tensor_copy(comp_own[:, :], own_count[:, :, 0])
            v.drain()
            bit = 0
            while (1 << bit) < W:
                k = 1 << bit
                a, b = shift[bit % 2], shift[(bit + 1) % 2]
                v.tensor_scalar(moved[:, :], a[:, :], k, None, ALU.bitwise_and)
                v.drain()
                v.scalar_tensor_tensor(out=b[:, :], in0=moved[:, :], scalar=0.0, in1=a[:, :],
                                       op0=ALU.is_equal, op1=ALU.mult)
                v.drain()
                v.copy_predicated(b[:, 0:W - k], moved[:, k:W], a[:, k:W])
                for t in (comp_src, comp_dst, comp_own):
                    v.copy_predicated(t[:, 0:W - k], moved[:, k:W], t[:, k:W])
                v.drain()
                bit += 1
            for k, comp in enumerate((comp_src, comp_dst, comp_own)):
                v.tensor_copy(packed[:, :, k], comp[:, :])
            v.tensor_scalar(spread[:, 0, :], upto[:, :], T.count[:, 0:1], None, ALU.mult)
            v.tensor_scalar(spread[:, 1, :], T.ident[:, :], T.count[:, 0:1], None, ALU.mult)
            v.drain()
            v.sem_inc(packed_made, 1)
            v.sem_inc(ready, 1)
            v.wait_ge(done, 3)
            v.tensor_copy(ends_row[:, :, :], T.psum[:, 4, 0:2 * P])
            v.tensor_scalar(lane0[:, :], lane_f[:, :], -float(S.N), None, ALU.add)
            v.drain()
            v.tensor_scalar(share_i[:, :], ends_row[:, 0, P - 1:P], float(P - 1), None, ALU.add)
            v.drain()
            v.tensor_scalar(share_i[:, :], share_i[:, :], P.bit_length() - 1, None, ALU.logical_shift_right)
            v.drain()
            v.tensor_copy(share[:, :], share_i[:, :])
            v.drain()
            first, old, skip, new_count = (deal[:, k:k + 1] for k in range(4))
            held_by = [deal[:, 4 + k:5 + k] for k in range(PARTS)]
            short, odd = deal[:, 8:9], deal[:, 9:10]
            v.tensor_tensor(first, lane0[:, :], share[:, :], ALU.mult)
            v.drain()
            v.tensor_scalar(pick[:, :], ends_row[:, 0, :], first, None, ALU.is_le)
            v.tensor_tensor(new_count, ends_row[:, 0, P - 1:P], first, ALU.subtract)
            v.drain()
            v.tensor_reduce(old, pick[:, :], AX.X, ALU.add)
            v.tensor_scalar(new_count, new_count, 0.0, share[:, 0:1], ALU.max, ALU.min)
            v.drain()
            v.tensor_tensor(pick[:, :], pick[:, :], ends_row[:, 1, :], ALU.mult)
            v.drain()
            v.tensor_reduce(skip, pick[:, :], AX.X, ALU.add)
            v.drain()
            v.tensor_tensor(skip, first, skip, ALU.subtract)
            for k in range(PARTS):
                v.tensor_scalar(odd, old, float(k), None, ALU.add)
                v.drain()
                v.tensor_scalar(pick[:, :], pos_f[:, 0:P], odd, None, ALU.is_equal)
                v.drain()
                v.tensor_tensor(pick[:, :], pick[:, :], ends_row[:, 1, :], ALU.mult)
                v.drain()
                v.tensor_reduce(held_by[k], pick[:, :], AX.X, ALU.add)
                v.drain()
            v.tensor_tensor(held_by[0], held_by[0], skip, ALU.subtract)
            v.drain()
            for k in range(1, PARTS):
                v.tensor_tensor(held_by[k], held_by[k], held_by[k - 1], ALU.add)
                v.drain()
            v.tensor_tensor(short, new_count, held_by[PARTS - 1], ALU.is_gt)
            v.drain()
            v.sem_inc(ready, 1)
            v.wait_ge(done, 4)
            v.tensor_scalar(odd, T.psum[:, 5, 0:1], 0.0, None, ALU.is_equal)
            v.drain()
            for value, kept in [(old, lane0[:, :]), (new_count, T.count[:, :])] + [(t, T.count[:, :]) for t in held_by]:
                v.tensor_tensor(value, value, kept, ALU.subtract)
                v.drain()
                v.scalar_tensor_tensor(out=value, in0=value, scalar=odd, in1=kept, op0=ALU.mult, op1=ALU.add)
            v.tensor_tensor(skip, skip, odd, ALU.mult)
            v.drain()
            v.tensor_copy(T.count[:, :], new_count)
            for k in range(PARTS):
                v.scalar_tensor_tensor(out=begin[:, k:k + 1], in0=old, scalar=float(W), in1=skip if k == 0 else held_by[k - 1],
                                       op0=ALU.mult, op1=ALU.add if k == 0 else ALU.subtract)
                v.drain()
                v.tensor_scalar(begin_i[:, k:k + 1], begin[:, k:k + 1], float(k * W), 3.0, ALU.add, ALU.mult)
            v.drain()
            v.sem_inc(ready, 1)
            v.sem_inc(begins_made, 1)
            v.wait_ge(parts_in, 16 * PARTS)
            for t, k in ((comp_src, 0), (comp_dst, 1), (comp_own, 2)):
                v.tensor_copy(t[:, :], part[0][:, :, k])
            for n in range(1, PARTS):
                v.tensor_scalar(tmp[:, :], pos_f[:, :], held_by[n - 1], None, ALU.is_ge)
                v.drain()
                for t, k in ((comp_src, 0), (comp_dst, 1), (comp_own, 2)):
                    v.copy_predicated(t[:, :], tmp[:, 0:W].bitcast(I32), part[n][:, :, k])
                v.drain()
            v.tensor_scalar(valid[:, :], pos_f[:, :], T.count[:, 0:1], None, ALU.is_lt)
            v.drain()
            for t, comp in ((T.src, comp_src), (T.dst, comp_dst)):
                v.memset(tmp[:, :], float(NONE))
                v.drain()
                v.copy_predicated(tmp[:, 0:W], valid[:, 0:W].bitcast(I32), comp[:, :])
                v.drain()
                v.tensor_tensor(t[:, 0:LW], tmp[:, :], valid[:, :], ALU.mult)
                v.drain()
            v.memset(T.start[:, :], 0.0)
            v.drain()
            v.tensor_tensor(T.start[:, 1:LW], tmp[:, 1:LW], tmp[:, 0:LW - 1], ALU.not_equal)
            v.drain()
            v.tensor_tensor(T.start[:, 0:LW], T.start[:, 0:LW], valid[:, :], ALU.mult)
            v.drain()
            v.tensor_scalar(T.low_start[:, 0:LW], T.start[:, 0:LW], LOW, None, ALU.mult)
            v.tensor_scalar(T.keep[:, :], T.start[:, 0:LW], -1.0, 1.0, ALU.mult, ALU.add)
            v.tensor_scalar(T.low_pad[:, 0:LW], valid[:, :], -LOW, LOW, ALU.mult, ALU.add)
            v.memset(T.own[:, :], 0.0)
            v.drain()
            v.copy_predicated(T.own[:, 0:W], valid[:, 0:W].bitcast(I32), comp_own[:, :])
            v.drain()
            v.scalar_tensor_tensor(out=T.low_own[:, :], in0=T.own[:, :], scalar=0.0, in1=valid[:, :],
                                   op0=ALU.is_equal, op1=ALU.mult)
            v.drain()
            v.tensor_scalar(T.low_own[:, :], T.low_own[:, :], LOW, None, ALU.mult)
            v.drain()
            v.tensor_tensor(T.low_own1[:, 0:LW], T.low_own[:, :], T.low_pad[:, 0:LW], ALU.add)
            v.tensor_scalar(is_head[:, :], tmp[:, :], tmp[:, 0:1], None, ALU.is_equal)
            v.drain()
            v.tensor_tensor(T.head_end[:, :], is_head[:, :], T.start[:, 1:LW + 1], ALU.mult)
            v.drain()
            v.tensor_reduce(T.has_head[:, :], T.head_end[:, :], AX.X, ALU.add)
            v.tensor_tensor(out_row_f[:, :], tmp[:, :], spare_f[:, :], ALU.subtract)
            v.drain()
            v.tensor_tensor(out_row_f[:, :], out_row_f[:, :], T.start[:, 1:LW + 1], ALU.mult)
            v.drain()
            v.tensor_tensor(T.out_row[:, :], out_row_f[:, :], spare_f[:, :], ALU.add)
            v.tensor_tensor(out_row_f[:, :], out_row_f[:, :], spare_f[:, :], ALU.add)
            v.drain()
            v.tensor_scalar(is_head[:, :], out_row_f[:, :], head_lane[:, 0:1], None, ALU.subtract)
            v.drain()
            v.tensor_tensor(is_head[:, :], is_head[:, :], T.head_end[:, :], ALU.mult)
            v.drain()
            v.tensor_tensor(T.out_row1[:, :], out_row_f[:, :], is_head[:, :], ALU.subtract)
            v.tensor_tensor(T.own_start[:, :], T.own[:, :], T.start[:, 0:LW], ALU.mult)
            v.tensor_tensor(valid[:, 0:LW - 1], valid[:, 0:LW - 1], valid[:, 1:LW], ALU.subtract)
            v.drain()
            v.tensor_tensor(valid[:, :], valid[:, :], tmp[:, :], ALU.mult)
            v.tensor_scalar(empty[:, :], T.count[:, :], 0.0, None, ALU.is_equal)
            v.drain()
            v.tensor_reduce(T.cross.keys[:, 0:1], valid[:, :], AX.X, ALU.add)
            v.drain()
            v.scalar_tensor_tensor(out=T.cross.keys[:, 0:1], in0=empty[:, :], scalar=float(NONE),
                                   in1=T.cross.keys[:, 0:1], op0=ALU.mult, op1=ALU.add)
            v.tensor_copy(T.cross.keys[:, 1:2], tmp[:, 0:1])
            v.drain()
            v.wait_ge(done, 5)
            v.tensor_reduce(most[:, 0:1], T.psum[0:1, 0, 0:P], AX.X, ALU.max)
            v.drain()
            v.tensor_scalar(begun[:, :], pos_f[0:1, 0:LW // EDGE_COLS], float(EDGE_COLS), most[:, 0:1], ALU.mult, ALU.is_lt)
            v.drain()
            v.tensor_reduce(most[:, :], begun[:, :], AX.X, ALU.add)
            v.drain()
            v.tensor_scalar(T.trips[:, :], most[:, :], 2.0, None, ALU.max)
            v.drain()
            T.cross.keys_dve(v, T.psum, ready, done, 6)
            v.tensor_scalar(linked[:, :], T.psum[:, 0, 0:P], T.cross.keys[:, 1:2], None, ALU.is_equal)
            v.drain()
            v.tensor_tensor(linked[:, :], linked[:, :], rank_mask[:, :], ALU.mult)
            v.drain()
            v.tensor_reduce(link[:, :], linked[:, :], AX.X, ALU.add)
            v.drain()
            v.tensor_scalar(link[:, :], link[:, :], 0.0, None, ALU.is_equal)
            v.drain()
            v.tensor_tensor(T.own_start[:, 0:1], T.own[:, 0:1], link[:, :], ALU.mult)
            v.tensor_tensor(rank_mask[:, :], rank_mask[:, :], T.cross.same_tt[:, :], ALU.mult)
            v.drain()
            v.tensor_reduce(tail_first[:, :], rank_mask[:, :], AX.X, ALU.add)
            v.drain()
            v.tensor_scalar(tail_first[:, :], tail_first[:, :], 0.0, None, ALU.is_equal)
            v.drain()
            v.tensor_tensor(empty[:, :], tail_first[:, :], empty[:, :], ALU.is_gt)
            v.drain()
            v.tensor_scalar(tail_first[:, :], T.cross.keys[:, 0:1], lane_f[:, 0:1], None, ALU.subtract)
            v.drain()
            v.tensor_tensor(tail_first[:, :], tail_first[:, :], empty[:, :], ALU.mult)
            v.drain()
            v.tensor_tensor(T.tail_row[:, :], tail_first[:, :], lane_f[:, :], ALU.add)
            v.tensor_reduce(link[:, :], T.cross.same_th[:, :], AX.X, ALU.add)
            v.drain()
            v.tensor_scalar(link[:, :], link[:, :], 0.0, None, ALU.is_equal)
            v.drain()
            v.tensor_tensor(tail_first[:, :], tail_first[:, :], link[:, :], ALU.mult)
            v.drain()
            v.tensor_tensor(T.last_row[:, 0:1], tail_first[:, :], lane_f[:, :], ALU.add)
            v.tensor_scalar(lane_f[:, :], lane_f[:, :], float(P), None, ALU.add)
            v.drain()
            v.tensor_tensor(link[:, :], T.cross.keys[:, 1:2], lane_f[:, :], ALU.subtract)
            v.drain()
            v.tensor_tensor(link[:, :], link[:, :], T.has_head[:, :], ALU.mult)
            v.drain()
            v.tensor_tensor(T.last_row[:, 1:2], link[:, :], lane_f[:, :], ALU.add)

            v.wait_ge(weights_loaded, 96)
            for k in range(2):
                v.wait_ge(att_loaded, 16 * (k + 1))
                for c in range(KC):
                    v.tensor_tensor(prod[:, :], w0[:, c, :], att_b[:, :], ALU.mult)
                    v.drain()
                    v.tensor_reduce(T.r0[:, c, S.IN + k * H0:S.IN + (k + 1) * H0],
                                    prod[:, :].rearrange("p (h c) -> p h c", h=H0), AX.X, ALU.add)
                    v.drain()
                v.sem_inc(att_used, 1)
            for c in range(KC):
                v.tensor_reduce(T.r0[:, c, 0:S.IN], w0[:, c, :].rearrange("p (h c) -> p c h", h=H0), AX.X, ALU.add)
            v.drain()
            v.tensor_scalar(T.r0[:, :, 0:S.IN], T.r0[:, :, 0:S.IN], 1.0 / H0, None, ALU.mult)
            v.drain()


class Cross:

    def __init__(s, nc, ctx, name, heads, keyed=None):
        s.nc, s.H = nc, heads

        def sb(n, sh, d=F32):
            return ctx.enter_context(nc.sbuf_tensor(f"{name}_{n}", sh, d))
        if keyed:
            s.same_tt, s.same_ht, s.same_th = keyed.same_tt, keyed.same_ht, keyed.same_th
        else:
            s.keys = sb("keys", [P, 2])
            s.head = sb("head_key", [P, 1])
            s.same_tt = sb("same_tt", [P, P])
            s.same_ht = sb("same_ht", [P, P])
            s.same_th = sb("same_th", [P, P])
        s.vals = sb("vals", [P, 2, heads])
        s.total = sb("total", [P, heads])
        s.before = sb("before", [P, heads])
        s.masked = sb("masked", [P, heads, P])
        s.part = sb("part", [P, heads])
        s.pen = sb("pen", [P, P])

    def keys_pe(s, psum, ident, ready, done, n):
        nc = s.nc
        nc.tensor.wait_ge(ready, n)
        nc.tensor.matmul(psum[:, 0, 0:P], s.keys[:, 0:1].broadcast_to([P, P]), ident[:, :], start=True, stop=True)
        nc.tensor.matmul(psum[:, 1, 0:P], s.head[:, :].broadcast_to([P, P]), ident[:, :],
                         start=True, stop=True).then_inc(done, 1)

    def keys_dve(s, v, psum, ready, done, n):
        v.tensor_tensor(s.head[:, :], s.keys[:, 0:1], s.keys[:, 1:2], ALU.is_equal)
        v.drain()
        v.scalar_tensor_tensor(out=s.head[:, :], in0=s.head[:, :], scalar=4.0 * NONE, in1=s.keys[:, 1:2],
                               op0=ALU.mult, op1=ALU.add)
        v.drain()
        v.sem_inc(ready, 1)
        v.wait_ge(done, n)
        v.tensor_scalar(s.same_tt[:, :], psum[:, 0, 0:P], s.keys[:, 0:1], None, ALU.is_equal)
        v.tensor_scalar(s.same_ht[:, :], psum[:, 0, 0:P], s.head[:, 0:1], None, ALU.is_equal)
        v.tensor_scalar(s.same_th[:, :], psum[:, 1, 0:P], s.keys[:, 0:1], None, ALU.is_equal)
        v.drain()

    def scans(s, v, op0, op1, left, values, fwd, bwd, low_start, n, begin, end):
        for h in range(s.H):
            v.tensor_tensor_scan(fwd[:, 0:n, h], left, values[h], begin(h), op0, op1)
        v.drain()
        for h in range(s.H):
            v.tensor_tensor_scan(bwd[:, 0:n, h][:, ::-1], low_start[:, 1:n + 1][:, ::-1], fwd[:, 0:n, h][:, ::-1],
                                 end(h), ALU.add, ALU.max)
        v.drain()

    def sums_pe(s, psum, ready, done, n):
        nc = s.nc
        nc.tensor.wait_ge(ready, n)
        nc.tensor.matmul(psum[:, 2, 0:s.H], s.same_tt[:, :], s.vals[:, 0, :], start=True, stop=False)
        nc.tensor.matmul(psum[:, 2, 0:s.H], s.same_ht[:, :], s.vals[:, 1, :], start=False, stop=True)
        nc.tensor.matmul(psum[:, 3, 0:s.H], s.same_th[:, :], s.vals[:, 0, :], start=True, stop=True).then_inc(done, 1)

    def sums_dve(s, v, psum, vals, fwd, bwd, keep, low_start, n, ready, done, k, values=None):
        vv = [values[:, 0:n] if values is not None else vals[:, 0:n, h] for h in range(s.H)]
        s.scans(v, ALU.mult, ALU.add, keep[:, 0:n], vv, fwd, bwd, low_start, n, lambda h: 0.0, lambda h: LOW)
        v.tensor_copy(s.vals[:, 0, :], fwd[:, n - 1, :])
        v.tensor_copy(s.vals[:, 1, :], bwd[:, 0, :])
        v.drain()
        v.sem_inc(ready, 1)
        v.wait_ge(done, k)
        v.tensor_copy(s.total[:, :], psum[:, 2, 0:s.H])
        v.tensor_copy(s.before[:, :], psum[:, 3, 0:s.H])
        v.drain()
        s.scans(v, ALU.mult, ALU.add, keep[:, 0:n], vv, fwd, bwd, low_start, n,
                lambda h: s.before[:, h:h + 1], lambda h: s.total[:, h:h + 1])

    def maxima_pe(s, psum, ident, ready, done, n):
        nc = s.nc
        nc.tensor.wait_ge(ready, n)
        for k in range(2):
            for h in range(s.H):
                at = psum[:, 2 * k + h // 4, (h % 4) * P:(h % 4 + 1) * P]
                mm = nc.tensor.matmul(at, s.vals[:, k, h:h + 1].broadcast_to([P, P]), ident[:, :],
                                      start=True, stop=True)
        mm.then_inc(done, 1)

    def maxima_dve(s, v, psum, vals, fwd, bwd, low_start, n, ready, done, k):
        vv = [vals[:, 0:n, h] for h in range(s.H)]
        s.scans(v, ALU.add, ALU.max, low_start[:, 0:n], vv, fwd, bwd, low_start, n, lambda h: LOW, lambda h: LOW)
        v.tensor_copy(s.vals[:, 0, :], fwd[:, n - 1, :])
        v.tensor_copy(s.vals[:, 1, :], bwd[:, 0, :])
        v.drain()
        s.join_maxima(v, psum, ready, done, k)
        s.scans(v, ALU.add, ALU.max, low_start[:, 0:n], vv, fwd, bwd, low_start, n,
                lambda h: s.before[:, h:h + 1], lambda h: s.total[:, h:h + 1])

    def join_maxima(s, v, psum, ready, done, k):
        v.sem_inc(ready, 1)
        v.wait_ge(done, k)
        for out, mask, bank in ((s.total, s.same_tt, 0), (s.part, s.same_th, 2), (s.before, s.same_ht, 0)):
            rows = psum[:, bank:bank + s.H // 4, :].rearrange("p b (h q) -> p (b h) q", q=P)
            v.tensor_scalar(s.pen[:, :], mask[:, :], -LOW, LOW, ALU.mult, ALU.add)
            v.drain()
            v.tensor_tensor(s.masked[:, :, :], rows,
                            s.pen[:, :].rearrange("p (o q) -> p o q", o=1).broadcast_to([P, s.H, P]), ALU.add)
            v.drain()
            v.tensor_reduce(out[:, :], s.masked[:, :, :], AX.X, ALU.max)
            v.drain()
        v.tensor_tensor(s.total[:, :], s.total[:, :], s.part[:, :], ALU.max)
        v.drain()


def after(eng, sem, i, per_step, offset, mark=None):
    if isinstance(i, int):
        if per_step * i + offset > 0:
            eng.wait_ge(sem, per_step * i + offset)
    elif mark is None:
        eng.wait_ge(sem, per_step * i + offset)
    else:
        held(eng, sem, per_step * i + offset, mark)


def node_pass(nc, S, T, layer, x, h=None, rows_out=None, base=None):
    N, KC, IN, B = S.N, S.KC, S.IN, BATCH
    R = (T.r0, T.r1)[layer]
    OUT = R.shape[2]
    lo = (IN, 0)[layer]
    rows = B * P
    steps = N // rows
    assert steps % SLOTS == 0 and 0 < N - steps * rows <= P, "one last tile covers the rest"
    trips = steps // SLOTS
    I = SLOTS * B
    end = I * trips
    with ExitStack() as ctx:
        def sb(n, s, d=F32):
            return ctx.enter_context(nc.sbuf_tensor(f"n{layer}_{n}", s, d))

        def sem(n):
            return ctx.enter_context(nc.semaphore(f"n{layer}_{n}"))
        xt = sb("x", [P, I, IN])
        ht = sb("h", [P, I, IN])
        bt = sb("base", [P, I, IN])
        ot = sb("out", [P, I, OUT - lo])
        hT = sb("hT", [P, SLOTS, KC, P])
        stats = sb("stats", [P, SLOTS, B, 6])
        mv = sb("mv", [P, SLOTS, B, 2])
        std = sb("std", [P, SLOTS, B])
        norm_by = sb("norm_by", [P, SLOTS, 2, B])
        zrow = sb("zrow", [P, IN])
        x_in = [sem(f"x_in{u}") for u in range(SLOTS)]
        moments = sem("moments")
        rooted = sem("rooted")
        scaled = sem("scaled")
        normed = sem("normed")
        based = sem("based")
        turned = sem("turned")
        copied = sem("copied")
        multiplied = sem("multiplied")
        evacuated = sem("evacuated")
        taken = sem("taken")
        h_st = [sem(f"h_stored{u}") for u in range(SLOTS)]
        rows_st = [sem(f"rows_stored{u}") for u in range(SLOTS)]
        base_st = [sem(f"base_stored{u}") for u in range(SLOTS)]
        zeroed = sem("zeroed")
        spare_st = sem("spare_stored")
        mark = {e: sem(f"mark_{e}") for e in ("sp", "act", "dve", "pool")}
        block = ctx.enter_context(nc.Block())
        GB = T.psum.shape[1] - SLOTS
        assert I % GB == 0

        def bank(n):
            return T.psum[:, n % GB, 0:OUT]

        def turn_bank(n):
            return T.psum[:, GB + n % SLOTS, 0:KC * P]

        def view(dram, s):
            return dram[bass.ds(s * rows, rows), :].rearrange("(p t) c -> p t c", t=B)

        def tile_rows(dram):
            return dram[N - P:N, :]

        def slot(u):
            return slice((u % SLOTS) * B, (u % SLOTS + 1) * B)

        def trip_loop(eng, body):
            for u in range(SLOTS):
                body(0, u)
            with eng.Fori(1, trips - 1) as i:
                for u in range(SLOTS):
                    body(i, u)
            for u in range(SLOTS):
                body(trips - 1, u)

        def behind(i, u, t, do):
            n = B * u + t - LAG
            if n >= 0:
                do(i, n // B, n % B)
            elif not (isinstance(i, int) and i == 0):
                do(i - 1, (n + I) // B, (n + I) % B)

        def inside(i, u):
            return not isinstance(i, int) or SLOTS * i + u < steps

        @block.sync
        def _(sp):
            sp.wait_ge(zeroed, 1)
            for k in range(SPARE // P):
                sp.dma_start(base[N + k * P:N + (k + 1) * P, :], zrow[:, :]).then_inc(spare_st, 16)

            def load(i, u):
                sp.dma_start(xt[:, slot(u), :], view(x, SLOTS * i + u)).then_inc(x_in[u % SLOTS], 16)

            def store_results(i, u):
                after(sp, taken, i, I, B * (u + 1), mark["sp"])
                sp.dma_start(view(rows_out, SLOTS * i + u), ot[:, slot(u), :]).then_inc(rows_st[u % SLOTS], 16)
                after(sp, evacuated, i, I, B * (u + 1), mark["sp"])
                sp.dma_start(view(base[0:N, :], SLOTS * i + u), bt[:, slot(u), :]).then_inc(base_st[u % SLOTS], 16)

            def body(i, u):
                after(sp, normed, i, I, B * (u + 1), mark["sp"])
                if layer == 0:
                    sp.dma_start(view(h, SLOTS * i + u), ht[:, slot(u), :]).then_inc(h_st[u], 16)
                if inside(i, u + SLOTS):
                    after(sp, based, i, SLOTS, u + 1, mark["sp"])
                    load(i + 1, u)
                if not (isinstance(i, int) and i == 0 and u == 0):
                    store_results(i, u - 1) if u else store_results(i - 1, SLOTS - 1)

            for u in range(SLOTS):
                load(0, u)
            trip_loop(sp, body)
            store_results(trips - 1, SLOTS - 1)
            sp.wait_ge(based, steps)
            sp.dma_start(xt[:, 0, :], tile_rows(x)).then_inc(x_in[0], 16)
            for u in range(SLOTS):
                sp.wait_ge(rows_st[u], 16 * trips)
                sp.wait_ge(base_st[u], 16 * trips)
                if layer == 0:
                    sp.wait_ge(h_st[u], 16 * trips)
            sp.wait_ge(normed, end + 1)
            if layer == 0:
                sp.dma_start(tile_rows(h), ht[:, 0, :]).then_inc(h_st[0], 16)
            sp.wait_ge(taken, end + 1)
            sp.dma_start(tile_rows(rows_out), ot[:, 0, :]).then_inc(rows_st[0], 16)
            sp.wait_ge(evacuated, end + 1)
            sp.dma_start(base[N - P:N, :], bt[:, 0, :]).then_inc(base_st[0], 16)
            sp.wait_ge(spare_st, 16 * (SPARE // P))
            sp.wait_ge(rows_st[0], 16 * (trips + 1))
            sp.wait_ge(base_st[0], 16 * (trips + 1))
            if layer == 0:
                sp.wait_ge(h_st[0], 16 * (trips + 1))

        @block.gpsimd
        def _(pool):
            def other(at, tiles):
                if layer == 0:
                    return T.bias_b[:, :].rearrange("p (o c) -> p o c", o=1).broadcast_to([P, tiles, IN])
                return ht[:, at, :]

            def body(i, u):
                after(pool, normed, i, I, B * (u + 1), mark["pool"])
                after(pool, base_st[u], i, 16, 0, mark["pool"])
                pool.tensor_tensor(bt[:, slot(u), :], xt[:, slot(u), :], other(slot(u), B), ALU.add).then_inc(based, 1)
            trip_loop(pool, body)
            pool.wait_ge(normed, end + 1)
            pool.wait_ge(base_st[0], 16 * trips)
            pool.tensor_tensor(bt[:, 0:1, :], xt[:, 0:1, :], other(slice(0, 1), 1), ALU.add).then_inc(based, 1)

        @block.scalar
        def _(act):
            def root(i, u):
                after(act, moments, i, SLOTS, u + 1, mark["act"])
                act.activation(std[:, u % SLOTS, :], mv[:, u % SLOTS, :, 1], ACT.Sqrt,
                               bias=T.eps[:, 0:1]).then_inc(rooted, 1)

            def norm(i, u, t):
                if t == 0:
                    after(act, scaled, i, SLOTS, u + 1, mark["act"])
                    if layer == 0:
                        after(act, h_st[u % SLOTS], i + u // SLOTS, 16, 0, mark["act"])
                    else:
                        after(act, based, i, SLOTS, u + 1 - SLOTS, mark["act"])
                k = (u % SLOTS) * B + t
                by = norm_by[:, u % SLOTS, :, t]
                act.activation(ht[:, k, :], xt[:, k, :], ACT.Relu, bias=by[:, 1:2],
                               scale=by[:, 0:1]).then_inc(normed, 1)

            def copy_turned(i, u, t):
                n = B * u + t
                after(act, turned, i, I, n + 1)
                after(act, multiplied, i, I, n + 1 - SLOTS)
                act.activation(hT[:, n % SLOTS, :, :], turn_bank(n), ACT.Copy).then_inc(copied, 1)

            def take_rows(i, u, t):
                n = B * u + t
                after(act, multiplied, i, I, n + 1, mark["act"])
                if t == 0:
                    after(act, rows_st[u], i, 16, 0, mark["act"])
                act.activation(ot[:, n, :], bank(n)[:, lo:OUT], ACT.Copy).then_inc(taken, 1)

            def body(i, u):
                for t in range(B):
                    copy_turned(i, u, t)
                    behind(i, u, t, take_rows)
                    if t == B - 1 and inside(i, u + 2):
                        root(i, u + 2)
                    if inside(i, u + 1):
                        norm(i, u + 1, t)

            root(0, 0)
            for t in range(B):
                norm(0, 0, t)
            root(0, 1)
            trip_loop(act, body)
            for n in range(LAG):
                behind(trips, 0, n, take_rows)
            act.wait_ge(moments, steps + 1)
            act.activation(std[:, 0, 0:1], mv[:, 0, 0:1, 1], ACT.Sqrt, bias=T.eps[:, 0:1]).then_inc(rooted, 1)
            act.wait_ge(scaled, steps + 1)
            if layer == 0:
                act.wait_ge(h_st[0], 16 * trips)
            else:
                act.wait_ge(based, steps)
            act.activation(ht[:, 0, :], xt[:, 0, :], ACT.Relu, bias=norm_by[:, 0, 1, 0:1],
                           scale=norm_by[:, 0, 0, 0:1]).then_inc(normed, 1)
            act.wait_ge(turned, end + 1)
            act.activation(hT[:, 0, :, :], turn_bank(0), ACT.Copy).then_inc(copied, 1)
            act.wait_ge(multiplied, end + 1)
            act.wait_ge(rows_st[0], 16 * trips)
            act.activation(ot[:, 0, :], bank(0)[:, lo:OUT], ACT.Copy).then_inc(taken, 1)

        @block.tensor
        def _(te):
            def products(n):
                for k in range(KC):
                    mm = nc.tensor.matmul(bank(n), hT[:, n % SLOTS, k, :], R[:, k, :], start=k == 0, stop=k == KC - 1)
                mm.then_inc(multiplied, 1)

            def turn(i, n):
                after(te, normed, i, I, n + 1)
                after(te, copied, i, I, n + 1 - SLOTS)
                for k in range(KC):
                    mm = nc.tensor.transpose(turn_bank(n)[:, k * P:(k + 1) * P],
                                             ht[:, n % I, k * P:(k + 1) * P], T.ident[:, :])
                mm.then_inc(turned, 1)

            def multiply(i, n):
                after(te, copied, i, I, n + 1)
                after(te, evacuated, i, I, n + 1 - GB)
                products(n)

            def body(i, u):
                for t in range(B):
                    n = B * u + t
                    if not (isinstance(i, int) and I * i + n + 1 >= end):
                        turn(i, n + 1)
                    multiply(i, n)
            turn(0, 0)
            trip_loop(te, body)
            te.wait_ge(normed, end + 1)
            for k in range(KC):
                mm = nc.tensor.transpose(turn_bank(0)[:, k * P:(k + 1) * P], ht[:, 0, k * P:(k + 1) * P], T.ident[:, :])
            mm.then_inc(turned, 1)
            te.wait_ge(copied, end + 1)
            te.wait_ge(evacuated, end)
            products(0)

        @block.vector
        def _(v):
            v.memset(zrow[:, :], 0.0).then_inc(zeroed, 1)

            def stats_of(i, u, t):
                if t == 0:
                    after(v, x_in[u % SLOTS], i + u // SLOTS, 16, 16, mark["dve"])
                v.bn_stats(stats[:, u % SLOTS, t, :], xt[:, (u % SLOTS) * B + t, :])

            def moments_of(u):
                v.drain()
                for t in range(B):
                    mm = v.bn_aggr(mv[:, u % SLOTS, t, :], stats[:, u % SLOTS, t, :])
                mm.then_inc(moments, 1)

            def scales_of(i, u):
                k = u % SLOTS
                after(v, normed, i, I, B * (u + 1) - I, mark["dve"])
                after(v, rooted, i, SLOTS, u + 1, mark["dve"])
                v.reciprocal(norm_by[:, k, 0, :], std[:, k, :])
                v.drain()
                v.scalar_tensor_tensor(out=norm_by[:, k, 1, :], in0=mv[:, k, :, 0], scalar=-1.0,
                                       in1=norm_by[:, k, 0, :], op0=ALU.mult, op1=ALU.mult).then_inc(scaled, 1)

            def evacuate(i, u, t):
                n = B * u + t
                after(v, taken, i, I, n + 1, mark["dve"])
                if t == 0:
                    after(v, based, i, SLOTS, u + 1, mark["dve"])
                v.tensor_tensor(bt[:, n, :], bank(n)[:, 0:IN], bt[:, n, :], ALU.add).then_inc(evacuated, 1)

            def body(i, u):
                if inside(i, u + 1) and not (isinstance(i, int) and i == 0 and u == 0):
                    scales_of(i, u + 1)
                for t in range(B):
                    behind(i, u, t, evacuate)
                    if inside(i, u + 2):
                        for k in range(2 * t, min(2 * t + 2, B)):
                            stats_of(i, u + 2, k)
                        if 2 * t < B <= 2 * t + 2:
                            moments_of(u + 2)

            for u in range(2):
                for t in range(B):
                    stats_of(0, u, t)
                moments_of(u)
                scales_of(0, u)
            trip_loop(v, body)
            for n in range(LAG):
                behind(trips, 0, n, evacuate)
            v.wait_ge(x_in[0], 16 * (trips + 1))
            v.wait_ge(normed, end)
            v.bn_stats(stats[:, 0, 0, :], xt[:, 0, :])
            v.drain()
            v.bn_aggr(mv[:, 0, 0, :], stats[:, 0, 0, :]).then_inc(moments, 1)
            v.wait_ge(rooted, steps + 1)
            v.reciprocal(norm_by[:, 0, 0, 0:1], std[:, 0, 0:1])
            v.drain()
            v.scalar_tensor_tensor(out=norm_by[:, 0, 1, 0:1], in0=mv[:, 0, 0:1, 0], scalar=-1.0,
                                   in1=norm_by[:, 0, 0, 0:1], op0=ALU.mult, op1=ALU.mult).then_inc(scaled, 1)
            v.wait_ge(taken, end + 1)
            v.wait_ge(based, steps + 1)
            v.tensor_tensor(bt[:, 0, :], bank(0)[:, 0:IN], bt[:, 0, :], ALU.add).then_inc(evacuated, 1)


class Scorer:

    def __init__(s, nc, ctx, S, T, logits):
        s.S, s.T, s.logits, s.G = S, T, logits, EDGE_COLS // 2

        def sb(n, sh, d=F32):
            return ctx.enter_context(nc.sbuf_tensor(f"score_{n}", sh, d))

        def sem(n):
            return ctx.enter_context(nc.semaphore(f"score_{n}"))
        s.ids = sb("ids", [P, 2, 2, s.G], I32)
        s.at_src = sb("at_src", [P, 2, s.G, 2 * S.H0])
        s.at_dst = sb("at_dst", [P, 2, s.G, 2 * S.H0])
        s.raw = sb("raw", [P, 2, s.G, S.H0])
        s.listed = sem("listed")
        s.gathered = [sem(f"gathered{b}") for b in range(2)]
        s.summed = sem("summed")
        s.marks = [sem(f"mark_{e}") for e in ("pool", "dve")]

    def pool(s, pool, trips):
        G, N, mark = s.G, s.S.N, s.marks[0]

        def gather(i, b):
            after(pool, s.listed, i, 4, 2 * (b + 1), mark)
            after(pool, s.summed, i, 2, b - 1, mark)
            for c in range(G):
                for k, t in enumerate((s.at_src, s.at_dst)):
                    pool.indirect_dma_start(
                        out=t[:, b, c, :], out_offset=None, in_=s.logits[:, :],
                        in_offset=bass.IndirectOffsetOnAxis(ap=s.ids[:, b, k, c:c + 1], axis=0),
                        bounds_check=N - 1, oob_is_err=False).then_inc(s.gathered[b], 16)

        def body(i):
            gather(i, 0)
            gather(i, 1)
        looped(pool, trips, body)

    def dve(s, v, trips, meanwhile):
        T, G, H, mark = s.T, s.G, s.S.H0, s.marks[1]

        def columns(i, b):
            return bass.ds((2 * i + b) * G, G)

        def index(i, b):
            for k, t in enumerate((T.src, T.dst)):
                v.tensor_copy(s.ids[:, b, k, :], t[:, columns(i, b)]).then_inc(s.listed, 1)

        def score(i, b):
            cols = columns(i, b)
            after(v, s.gathered[b], i, 32 * G, 32 * G, mark)
            v.tensor_tensor(s.raw[:, 0, :, :], s.at_src[:, b, :, 0:H], s.at_dst[:, b, :, H:2 * H], ALU.add)
            v.tensor_tensor(s.raw[:, 1, :, :], s.at_dst[:, b, :, 0:H], s.at_dst[:, b, :, H:2 * H], ALU.add)
            v.drain().then_inc(s.summed, 1)
            for k, t in enumerate((T.score, T.score_own)):
                v.scalar_tensor_tensor(out=t[:, cols, :], in0=s.raw[:, k, :, :], scalar=SLOPE, in1=s.raw[:, k, :, :],
                                       op0=ALU.mult, op1=ALU.max)
            v.drain()
            v.tensor_tensor(T.score[:, cols, :], T.score[:, cols, :], last(T.low_pad[:, cols], H), ALU.add)
            v.tensor_tensor(T.score_own[:, cols, :], T.score_own[:, cols, :], last(T.low_own[:, cols], H), ALU.add)
            v.drain()

        def body(i):
            for b in range(2):
                score(i, b)
                index(i + 1, b)
        index(0, 0)
        index(0, 1)
        v.memset(T.score[:, :, :], LOW)
        v.memset(T.score_own[:, :, :], 0.0)
        meanwhile()
        v.drain()
        looped(v, trips, body)


def softmax(nc, S, T, logits, W0, attn_s, attn_d):
    H, LW = S.H0, S.LW
    cross, score, own = T.cross, T.score, T.score_own
    step = EDGE_COLS
    with ExitStack() as ctx:
        fwd = ctx.enter_context(nc.sbuf_tensor("fwd0", [P, LW, H], F32))
        bwd = ctx.enter_context(nc.sbuf_tensor("bwd0", [P, LW, H], F32))
        ready = ctx.enter_context(nc.semaphore("softmax_rows_ready"))
        done = ctx.enter_context(nc.semaphore("softmax_matmuls_done"))
        scorer = Scorer(nc, ctx, S, T, logits)
        w0 = ctx.enter_context(nc.sbuf_tensor("w0_again", [P, S.KC, S.H0 * S.C0], F32))
        att_b = ctx.enter_context(nc.sbuf_tensor("att_b1", [P, 2, S.IN], F32))
        prod = ctx.enter_context(nc.sbuf_tensor("prod1", [P, S.IN], F32))
        weights_loaded = ctx.enter_context(nc.semaphore("weights_loaded_again"))
        shifted = ctx.enter_context(nc.semaphore("shifted"))
        exped = ctx.enter_context(nc.semaphore("exped"))
        block = ctx.enter_context(nc.Block())
        few = -(-(S.E - S.N) // (P * step)) * step

        def by_width(eng, trips, run):
            with eng.If(trips < few // step + 1):
                run(few)
            with eng.If(trips > few // step):
                run(LW)

        @block.sync
        def _(sp):
            sp.dma_start(w0[:, :, :], W0.rearrange("(k p) n -> p k n", p=P)).then_inc(weights_loaded, 16)
            for k, vec in enumerate((attn_s, attn_d)):
                sp.dma_start(att_b[:, k, :], vec.partition_broadcast(P)).then_inc(weights_loaded, 16)
            sp.wait_ge(weights_loaded, 48)

        @block.gpsimd
        def _(pool):
            scorer.pool(pool, pool.value_load(T.trips[0:1, 0:1], min_val=2, max_val=LW // step))

        @block.tensor
        def _(te):
            cross.maxima_pe(T.psum, T.ident, ready, done, 1)
            cross.sums_pe(T.psum, ready, done, 2)

        @block.scalar
        def _(act):
            def run(n):
                act.wait_ge(shifted, 1)
                act.activation(score[:, 0:n, :], score[:, 0:n, :], ACT.Exp).then_inc(exped, 1)
                act.activation(own[:, 0:n, :], own[:, 0:n, :], ACT.Exp).then_inc(exped, 1)
            by_width(act, act.value_load(T.trips[0:1, 0:1], min_val=2, max_val=LW // step), run)

        @block.vector
        def _(v):
            def run(n):
                cross.maxima_dve(v, T.psum, score, fwd, bwd, T.low_start, n, ready, done, 1)
                v.tensor_tensor(bwd[:, 0:n, :], bwd[:, 0:n, :], own[:, 0:n, :], ALU.max)
                v.drain()
                v.tensor_tensor(score[:, 0:n, :], score[:, 0:n, :], bwd[:, 0:n, :], ALU.subtract)
                v.tensor_tensor(own[:, 0:n, :], own[:, 0:n, :], bwd[:, 0:n, :], ALU.subtract).then_inc(shifted, 1)
                v.wait_ge(exped, 2)
                cross.sums_dve(v, T.psum, score, fwd, bwd, T.keep, T.low_start, n, ready, done, 2)
                v.tensor_tensor(own[:, 0:n, :], own[:, 0:n, :], last(T.own[:, 0:n], H), ALU.mult)
                v.drain()
                v.tensor_tensor(bwd[:, 0:n, :], bwd[:, 0:n, :], own[:, 0:n, :], ALU.add)
                v.drain()
                v.tensor_scalar(bwd[:, 0:n, :], bwd[:, 0:n, :], 1e-16, None, ALU.add)
                v.drain()
                v.reciprocal(bwd[:, 0:n, :], bwd[:, 0:n, :])
                v.drain()
                v.scalar_tensor_tensor(out=T.alpha[:, 0:n, :], in0=score[:, 0:n, :], scalar=1.0 / H,
                                       in1=bwd[:, 0:n, :], op0=ALU.mult, op1=ALU.mult)
                v.drain()

            def split_weights():
                v.wait_ge(weights_loaded, 48)
                v.tensor_copy(T.w_high[:, :, :], w0[:, :, :])
                v.drain()
                v.tensor_tensor(T.w_low[:, :, :], w0[:, :, :], T.w_high[:, :, :].bitcast(F32), ALU.subtract)
                for k in range(2):
                    for c in range(S.KC):
                        m = P if c < S.KC - 1 else S.CON - P
                        v.tensor_tensor(prod[0:m, :], T.r1[0:m, c, 0:S.IN], att_b[0:m, k, :], ALU.mult)
                        v.drain()
                        v.tensor_reduce(T.r1[0:m, c, S.IN + k * S.H1:S.IN + (k + 1) * S.H1],
                                        prod[0:m, :].rearrange("p (h c) -> p h c", h=S.H1), AX.X, ALU.add)
                        v.drain()
                v.drain()

            trips = v.value_load(T.trips[0:1, 0:1], min_val=2, max_val=LW // step)
            scorer.dve(v, trips, split_weights)
            by_width(v, trips, run)


class Rows:

    def __init__(s, nc, ctx, S, T, name, K, width, per, dve_indexes=False):
        s.dve_indexes = dve_indexes
        s.S, s.T, s.K, s.HALF, s.per = S, T, K, K // 2, per

        def sb(n, sh, d=F32):
            return ctx.enter_context(nc.sbuf_tensor(f"{name}_{n}", sh, d))

        def sem(n):
            return ctx.enter_context(nc.semaphore(f"{name}_{n}"))
        s.ids = sb("ids", [P, 2, 2, K // 2], I32)
        s.outs = sb("outs", [P, 2, K // 2], I32)
        s.rows_s = sb("rows_s", [P, K, width])
        s.rows_d = sb("rows_d", [P, K, width])
        s.out = sb("out", [P, K, S.IN])
        s.cleared = sem("cleared")
        s.listed = sem("listed")
        s.out_listed = sem("out_listed")
        s.gathered = [sem(f"gathered{b}") for b in range(2)]
        s.used = sem("used")
        s.summed = sem("summed")
        s.added = [sem(f"added{k}") for k in range(2 * per)]
        s.mark = sem("mark_rows")

    def landed(s, v, i, b, mark):
        after(v, s.gathered[b], i, 16 * s.K, 16 * s.K, mark)

    def index(s, v, i, b):
        for k, t in enumerate((s.T.src, s.T.dst)):
            v.tensor_copy(s.ids[:, b, k, :], t[:, bass.ds((2 * i + b) * s.HALF, s.HALF)]).then_inc(s.listed, 1)

    def index_out(s, v, i, b, out_row):
        return v.tensor_copy(s.outs[:, b, :], out_row[:, bass.ds((2 * i + b) * s.HALF, s.HALF)])

    def run(s, pool, trips, feat, base, out_row):
        T, K, HALF, N = s.T, s.K, s.HALF, s.S.N

        def gather(i, b):
            after(pool, s.used, i, 2 * s.per, s.per * (b - 1), s.mark)
            if not s.dve_indexes:
                s.index(pool, i, b)
            after(pool, s.listed, i, 4, 2 * (b + 1), s.mark)
            for c in range(HALF):
                for k, t in enumerate((s.rows_s, s.rows_d)):
                    pool.indirect_dma_start(
                        out=t[:, b * HALF + c, :], out_offset=None, in_=feat[:, :],
                        in_offset=bass.IndirectOffsetOnAxis(ap=s.ids[:, b, k, c:c + 1], axis=0),
                        bounds_check=N - 1, oob_is_err=False).then_inc(s.gathered[b], 16)

        def scatter(i, b):
            if not s.dve_indexes:
                for c in range(s.per):
                    after(pool, s.added[b * s.per + c], i, 16 * HALF // s.per, 0, s.mark)
                s.index_out(pool, i, b, out_row).then_inc(s.out_listed, 1)
                after(pool, s.out_listed, i, 2, b + 1, s.mark)
            for c in range(HALF):
                k = b * HALF + c
                if c < s.per:
                    after(pool, s.summed, i, 2 * s.per, s.per * b + c + 1, s.mark)
                pool.indirect_dma_start(
                    out=base[:, :], out_offset=bass.IndirectOffsetOnAxis(ap=s.outs[:, b, c:c + 1], axis=0),
                    in_=s.out[:, k, :], in_offset=None, bounds_check=N + SPARE - 1, oob_is_err=True,
                    compute_op=ALU.add).then_inc(s.added[b * s.per + c % s.per], 16)

        gather(0, 0)

        def body(i):
            gather(i, 1)
            scatter(i, 0)
            gather(i + 1, 0)
            scatter(i, 1)
        looped(pool, trips, body)
        for sem in s.added:
            held(pool, sem, 16 * HALF // s.per * trips, s.mark)
        held(pool, s.gathered[0], 16 * K * (trips + 1), s.mark)

    def add_last(s, pool, base, rows, values, sem):
        return pool.indirect_dma_start(
            out=base[:, :], out_offset=bass.IndirectOffsetOnAxis(ap=rows, axis=0), in_=values, in_offset=None,
            bounds_check=s.S.N + SPARE - 1, oob_is_err=True, compute_op=ALU.add).then_inc(sem, 16)


def edge_pass0(nc, S, T, feat, base):
    H, K, HALF, IN, KC = S.H0, EDGE_COLS, EDGE_COLS // 2, S.IN, S.KC
    BANKS = H * S.C0 // BANK
    PER = BANK // S.C0
    limit = S.LW // K
    with ExitStack() as ctx:
        def sb(n, s, d=F32):
            return ctx.enter_context(nc.sbuf_tensor(f"e0_{n}", s, d))

        def sem(n):
            return ctx.enter_context(nc.semaphore(f"e0_{n}"))
        R = Rows(nc, ctx, S, T, "e0", K, IN, HALF)
        diff = sb("diff", [P, 2, IN])
        high = sb("high", [P, 2, KC, P], F32R)
        low = sb("low", [P, 2, KC, P], F32R)
        first = sb("first", [P, 2, IN])
        wts = sb("wts", [P, 2, HALF, H + 1])
        tails = sb("tails", [P, IN])
        turned = sem("turned")
        copied = sem("copied")
        lowered = sem("lowered")
        multiplied = sem("multiplied")
        weighted = sem("weighted")
        took = sem("took")
        tails_made = sem("tails_made")
        tails_added = sem("tails_added")
        weights_in = sem("weights_in")
        mark = {e: sem(f"mark_{e}") for e in ("dve", "act", "pe")}
        block = ctx.enter_context(nc.Block())
        cleared = R.cleared

        @block.gpsimd
        def _(pool):
            trips = pool.value_load(T.trips[0:1, 0:1], min_val=2, max_val=limit)
            R.run(pool, trips, feat, base, T.out_row)
            pool.wait_ge(tails_made, 2)
            R.add_last(pool, base, T.tail_row[:, 0:1], tails[:, :], tails_added)
            pool.wait_ge(tails_added, 16)

        @block.tensor
        def _(te):
            te.wait_ge(cleared, 1)
            trips = te.value_load(T.trips[0:1, 0:1], min_val=2, max_val=limit)

            def turn(i, k):
                after(te, R.used, i, K, k + 1)
                after(te, lowered, i, K, k - 1)
                for c in range(KC):
                    mm = nc.tensor.transpose(T.psum[:, 6 + k % 2, c * P:(c + 1) * P],
                                             diff[:, k % 2, c * P:(c + 1) * P], T.ident[:, :])
                mm.then_inc(turned, 1)

            def multiply(i, k, u):
                if u == 0:
                    after(te, lowered, i, K, k + 1)
                after(te, took, i, BANKS * K, BANKS * (k - 1) + u + 1)
                parts = [(high, T.w_high), (high, T.w_low), (low, T.w_high)]
                for c in range(KC):
                    for n, (d, w) in enumerate(parts):
                        mm = nc.tensor.matmul(T.psum[:, u, :], d[:, k % 2, c, :], w[:, c, u * BANK:(u + 1) * BANK],
                                              start=c == 0 and n == 0, stop=c == KC - 1 and n == 2)
                mm.then_inc(multiplied, 1)

            def body(i):
                for k in range(K):
                    for u in range(BANKS):
                        if u == BANKS // 2:
                            turn(i, k + 1) if k < K - 1 else turn(i + 1, 0)
                        multiply(i, k, u)
            turn(0, 0)
            looped(te, trips, body)
            te.wait_ge(tails_made, 1)
            nc.tensor.matmul(T.psum[:, 5, 0:IN], T.cross.same_tt[:, :], R.out[:, K - 1, :],
                             start=True, stop=True).then_inc(turned, 1)

        @block.scalar
        def _(act):
            act.wait_ge(cleared, 1)
            trips = act.value_load(T.trips[0:1, 0:1], min_val=2, max_val=limit)

            def part(i, k):
                after(act, turned, i, K, k + 1, mark["act"])
                after(act, multiplied, i, BANKS * K, BANKS * (k - 1), mark["act"])
                act.activation(high[:, k % 2, :, :], T.psum[:, 6 + k % 2, 0:KC * P], ACT.Copy).then_inc(copied, 1)

            def body(i):
                for k in range(K):
                    after(act, multiplied, i, BANKS * K, BANKS * k + 1, mark["act"])
                    after(act, weights_in, i, 2, k // HALF + 1, mark["act"])
                    after(act, R.summed, i, K, k - 1, mark["act"])
                    act.activation(first[:, k % 2, :], T.psum[:, 0, 0:S.C0], ACT.Copy,
                                   scale=wts[:, k // HALF, k % HALF, 0:1]).then_inc(weighted, 1)
                    part(i, k + 1) if k < K - 1 else part(i + 1, 0)
            part(0, 0)
            looped(act, trips, body)

        @block.vector
        def _(v):
            v.memset(R.out[:, K - 1, :], 0.0)
            v.drain().then_inc(cleared, 1)
            trips = v.value_load(T.trips[0:1, 0:1], min_val=2, max_val=limit)

            def differ(i, k):
                if k % HALF == 0:
                    R.landed(v, i, k // HALF, mark["dve"])
                after(v, turned, i, K, k - 1, mark["dve"])
                v.tensor_tensor(diff[:, k % 2, :], R.rows_s[:, k, :], R.rows_d[:, k, :],
                                ALU.subtract).then_inc(R.used, 1)

            def lower(i, k):
                after(v, copied, i, K, k + 1, mark["dve"])
                after(v, multiplied, i, BANKS * K, BANKS * (k - 1), mark["dve"])
                v.tensor_tensor(low[:, k % 2, :, :],
                                T.psum[:, 6 + k % 2, 0:KC * P].rearrange("p (c q) -> p c q", c=KC),
                                high[:, k % 2, :, :].bitcast(F32), ALU.subtract).then_inc(lowered, 1)

            def take_weights(i, b):
                after(v, weighted, i, K, HALF * (b + 1) - K, mark["dve"])
                at = bass.ds((2 * i + b) * HALF, HALF)
                v.tensor_copy(wts[:, b, :, 0:H], T.alpha[:, at, :])
                v.tensor_copy(wts[:, b, :, H], T.keep[:, at])
                v.drain().then_inc(weights_in, 1)

            def body(i):
                for k in range(K):
                    if k % HALF == 0:
                        take_weights(i, k // HALF)
                    w = wts[:, k // HALF, k % HALF, :]
                    out = R.out[:, k, :]
                    differ(i, k + 1) if k < K - 1 else differ(i + 1, 0)
                    after(v, R.added[k], i, 16, 0, mark["dve"])
                    after(v, weighted, i, K, k + 1, mark["dve"])
                    v.scalar_tensor_tensor(out=out, in0=R.out[:, (k - 1) % K, :], scalar=w[:, H:H + 1],
                                           in1=first[:, k % 2, :], op0=ALU.mult, op1=ALU.add)
                    for h in range(1, H):
                        if h == 2 * PER:
                            lower(i, k + 1) if k < K - 1 else lower(i + 1, 0)
                        if h % PER == 0:
                            after(v, multiplied, i, BANKS * K, BANKS * k + h // PER + 1, mark["dve"])
                        v.drain()
                        mm = v.scalar_tensor_tensor(
                            out=out, in0=T.psum[:, h // PER, (h % PER) * S.C0:(h % PER + 1) * S.C0],
                            scalar=w[:, h:h + 1], in1=out, op0=ALU.mult, op1=ALU.add)
                        if h % PER == PER - 1:
                            mm.then_inc(took, 1)
                    v.drain().then_inc(R.summed, 1)
            differ(0, 0)
            lower(0, 0)
            looped(v, trips, body)
            v.drain().then_inc(tails_made, 1)
            held(v, turned, K * trips + 2, mark["dve"])
            v.tensor_copy(tails[:, :], T.psum[:, 5, 0:IN]).then_inc(tails_made, 1)


def edge_pass1(nc, S, T, feat, base):
    H, K, IN, D = S.H1, EDGE_COLS, S.IN, S.D1
    HALF = K // 2
    limit = S.LW // K
    WIDE = IN + H
    with ExitStack() as ctx:
        def sb(n, s, d=F32):
            return ctx.enter_context(nc.sbuf_tensor(f"e1_{n}", s, d))

        def sem(n):
            return ctx.enter_context(nc.semaphore(f"e1_{n}"))
        R = Rows(nc, ctx, S, T, "e1", K, IN + 2 * H, 1, dve_indexes=True)
        scaled = sb("scaled", [P, IN, HALF + 1])
        factor = sb("factor", [P, IN, HALF + 1])
        acc = sb("acc", [P, IN, HALF + 1])
        low = sb("low", [P, H, HALF + 1])
        raw = sb("raw", [P, 2, H, HALF])
        biased = sb("biased", [P, 2, H, HALF])
        top = sb("top", [P, H, HALF + 1])
        m = sb("m", [P, H, HALF + 1])
        gain = sb("gain", [P, H, HALF + 1])
        l = sb("l", [P, H, HALF + 1])
        args = sb("args", [P, 3, H, HALF + 1])
        exps = sb("exps", [P, 3, H, HALF + 1])
        own_gain = sb("own_gain", [P, H, HALF])
        inv = sb("inv", [P, H, HALF])
        pick = sb("pick", [P, 2, H, HALF])
        picked = sb("picked", [P, 2, H])
        head_acc = sb("head_acc", [P, IN])
        head_ml = sb("head_ml", [P, 2, H])
        tail_ml = sb("tail_ml", [P, 2, H])
        no_head = sb("no_head", [P, 1])
        top_of = sb("top_of", [P, 2, H])
        scale = sb("scale", [P, 2, H])
        wide = sb("wide", [P, 2, WIDE])
        joint = sb("joint", [P, 2, WIDE])
        last_out = sb("last_out", [P, 2, IN])
        maxed = sem("maxed")
        exped = sem("exped")
        ready = sem("ready")
        done = sem("done")
        heads_back = sem("heads_back")
        lasts_made = sem("lasts_made")
        lasts_added = sem("lasts_added")
        mark = {e: sem(f"mark_{e}") for e in ("dve", "act")}
        block = ctx.enter_context(nc.Block())
        cross = T.cross1

        def heads(ap):
            return ap.rearrange("p (h d) -> p h d", h=H)

        def over_head(ap):
            return ap.rearrange("p h (o c) -> p h o c", o=1).broadcast_to([P, H, D, ap.shape[2]])

        def over_heads(ap):
            return ap.rearrange("p (o c) -> p o c", o=1).broadcast_to([P, H, ap.shape[1]])

        def flat(ap):
            return ap.rearrange("p f c -> p (f c)")

        @block.gpsimd
        def _(pool):
            trips = pool.value_load(T.trips[0:1, 0:1], min_val=2, max_val=limit)
            R.run(pool, trips, feat, base, T.out_row1)
            pool.dma_start(head_acc[:, :], base[S.N + HEADS_AT:S.N + SPARE, :]).then_inc(heads_back, 16)
            pool.wait_ge(lasts_made, 1)
            for k in range(2):
                R.add_last(pool, base, T.last_row[:, k:k + 1], last_out[:, k, :], lasts_added)
            pool.wait_ge(lasts_added, 32)

        @block.scalar
        def _(act):
            act.wait_ge(R.cleared, 1)
            trips = act.value_load(T.trips[0:1, 0:1], min_val=2, max_val=limit)

            def exp(i, b):
                after(act, maxed, i, 2, b + 1, mark["act"])
                act.activation(exps[:, :, :, :], args[:, :, :, :], ACT.Exp).then_inc(exped, 1)
                act.activation(factor[:, :, :].rearrange("p (h d) c -> p h d c", h=H), over_head(args[:, 2, :, :]),
                               ACT.Exp).then_inc(exped, 1)

            def body(i):
                exp(i, 0)
                exp(i, 1)
            looped(act, trips, body)
            held(act, maxed, 2 * trips + 1, mark["act"])
            act.activation(scale[:, :, :], top_of[:, :, :], ACT.Exp).then_inc(exped, 1)

        @block.tensor
        def _(te):
            cross.maxima_pe(T.psum, T.ident, ready, done, 1)
            te.wait_ge(ready, 2)
            nc.tensor.matmul(T.psum[:, 4, 0:WIDE], cross.same_tt[:, :], wide[:, 0, :], start=True, stop=False)
            nc.tensor.matmul(T.psum[:, 4, 0:WIDE], cross.same_ht[:, :], wide[:, 1, :], start=False, stop=True)
            nc.tensor.matmul(T.psum[:, 5, 0:WIDE], cross.same_th[:, :], wide[:, 0, :],
                             start=True, stop=True).then_inc(done, 1)

        @block.vector
        def _(v):
            R.index(v, 0, 0)
            R.index(v, 0, 1)
            v.memset(acc[:, :, :], 0.0)
            v.memset(m[:, :, :], LOW)
            v.memset(l[:, :, :], 0.0)
            v.memset(head_ml[:, :, :], 0.0)
            v.memset(args[:, :, :, :], LOW)
            v.memset(low[:, :, :], LOW)
            v.drain().then_inc(R.cleared, 1)
            trips = v.value_load(T.trips[0:1, 0:1], min_val=2, max_val=limit)

            def by_head(ap):
                return ap.rearrange("p c h -> p h c")

            def by_feature(ap):
                return ap.rearrange("p c (h d) -> p h d c", h=H)

            def split(ap):
                return ap.rearrange("p (h d) c -> p h d c", h=H)

            def half(i, b):
                R.landed(v, i, b, mark["dve"])
                R.index(v, i + 1, b)
                cols = bass.ds((2 * i + b) * HALF, HALF)
                rows = slice(b * HALF, (b + 1) * HALF)
                new = slice(1, HALF + 1)
                s_src = by_head(R.rows_s[:, rows, IN:IN + H])
                d_src, d_dst = by_head(R.rows_d[:, rows, IN:IN + H]), by_head(R.rows_d[:, rows, IN + H:IN + 2 * H])
                v.tensor_tensor(raw[:, 0, :, :], s_src, d_dst, ALU.add)
                v.tensor_tensor(raw[:, 1, :, :], d_src, d_dst, ALU.add)
                v.tensor_copy(top[:, :, 0:1], m[:, :, HALF:])
                v.tensor_copy(low[:, :, new], over_heads(T.low_start[:, cols]))
                v.drain()
                v.scalar_tensor_tensor(out=biased[:, :, :, :].rearrange("p a h c -> p (a h c)"),
                                       in0=raw[:, :, :, :].rearrange("p a h c -> p (a h c)"), scalar=SLOPE,
                                       in1=raw[:, :, :, :].rearrange("p a h c -> p (a h c)"),
                                       op0=ALU.mult, op1=ALU.max)
                v.drain()
                v.tensor_tensor(biased[:, 0, :, :], biased[:, 0, :, :], over_heads(T.low_pad[:, cols]), ALU.add)
                v.tensor_tensor(biased[:, 1, :, :], biased[:, 1, :, :], over_heads(T.low_own1[:, cols]), ALU.add)
                v.drain()
                v.tensor_tensor(top[:, :, new], biased[:, 0, :, :], biased[:, 1, :, :], ALU.max)
                v.drain()
                v.tensor_tensor_scan(flat(m[:, :, :]), flat(low[:, :, :]), flat(top[:, :, :]), LOW, ALU.add, ALU.max)
                v.drain()
                for k in range(2):
                    v.tensor_tensor(args[:, k, :, new], biased[:, k, :, :], m[:, :, new], ALU.subtract)
                v.tensor_tensor(args[:, 2, :, new], m[:, :, 0:HALF], m[:, :, new], ALU.subtract)
                v.drain()
                v.tensor_tensor(args[:, 2, :, new], args[:, 2, :, new], low[:, :, new], ALU.add)
                v.drain().then_inc(maxed, 1)
                v.tensor_tensor(split(scaled[:, :, new]), by_feature(R.rows_s[:, rows, 0:IN]),
                                by_feature(R.rows_d[:, rows, 0:IN]), ALU.subtract).then_inc(R.used, 1)
                v.tensor_copy(scaled[:, :, 0:1], acc[:, :, HALF:])
                v.tensor_copy(gain[:, :, 0:1], l[:, :, HALF:])
                after(v, exped, i, 4, 2 * (b + 1), mark["dve"])
                v.tensor_tensor(own_gain[:, :, :], exps[:, 1, :, new], over_heads(T.own_start[:, cols]), ALU.mult)
                v.drain()
                v.tensor_tensor(split(scaled[:, :, new]), split(scaled[:, :, new]), over_head(exps[:, 0, :, new]), ALU.mult)
                v.tensor_tensor(gain[:, :, new], own_gain[:, :, :], exps[:, 0, :, new], ALU.add)
                v.drain()
                v.tensor_tensor_scan(flat(l[:, :, :]), flat(exps[:, 2, :, :]), flat(gain[:, :, :]), 0.0, ALU.mult, ALU.add)
                v.tensor_tensor_scan(flat(acc[:, :, :]), flat(factor[:, :, :]), flat(scaled[:, :, :]), 0.0, ALU.mult, ALU.add)
                v.drain()
                v.tensor_scalar(inv[:, :, :], l[:, :, new], 1e-30, None, ALU.max)
                v.tensor_tensor(pick[:, 0, :, :], m[:, :, new], over_heads(T.head_end[:, cols]), ALU.mult)
                v.tensor_tensor(pick[:, 1, :, :], l[:, :, new], over_heads(T.head_end[:, cols]), ALU.mult)
                v.drain()
                v.reciprocal(inv[:, :, :], inv[:, :, :])
                for k in range(2):
                    v.tensor_reduce(picked[:, k, :], pick[:, k, :, :], AX.X, ALU.add)
                after(v, R.added[b], i, 16 * HALF, 0, mark["dve"])
                R.index_out(v, i, b, T.out_row1)
                v.drain()
                v.tensor_tensor(by_feature(R.out[:, rows, :]), split(acc[:, :, new]), over_head(inv[:, :, :]),
                                ALU.mult).then_inc(R.summed, 1)
                v.tensor_tensor(head_ml[:, :, :], head_ml[:, :, :], picked[:, :, :], ALU.add)

            def body(i):
                half(i, 0)
                half(i, 1)
            looped(v, trips, body)
            v.drain()
            v.tensor_copy(tail_ml[:, 0, :], m[:, :, HALF])
            v.tensor_copy(tail_ml[:, 1, :], l[:, :, HALF])
            v.tensor_scalar(no_head[:, :], T.has_head[:, :], -LOW, LOW, ALU.mult, ALU.add)
            v.drain()
            v.tensor_copy(cross.vals[:, 0, :], tail_ml[:, 0, :])
            v.tensor_scalar(cross.vals[:, 1, :], head_ml[:, 0, :], no_head[:, 0:1], None, ALU.add)
            v.drain()
            cross.join_maxima(v, T.psum, ready, done, 1)
            v.tensor_copy(top_of[:, 0, :], cross.total[:, :])
            v.tensor_tensor(top_of[:, 1, :], cross.before[:, :], cross.vals[:, 1, :], ALU.max)
            v.drain()
            v.tensor_tensor(top_of[:, :, :], cross.vals[:, :, :], top_of[:, :, :], ALU.subtract)
            v.drain().then_inc(maxed, 1)
            held(v, exped, 4 * trips + 1, mark["dve"])
            v.wait_ge(heads_back, 16)
            v.tensor_tensor(heads(head_acc[:, :]), heads(head_acc[:, :]), last(head_ml[:, 1, :], D), ALU.mult)
            v.drain()
            for k, (a, ml) in enumerate(((acc[:, :, HALF], tail_ml), (head_acc[:, :], head_ml))):
                v.tensor_tensor(heads(wide[:, k, 0:IN]), heads(a), last(scale[:, k, :], D), ALU.mult)
                v.tensor_tensor(wide[:, k, IN:WIDE], ml[:, 1, :], scale[:, k, :], ALU.mult)
            v.drain().then_inc(ready, 1)
            v.wait_ge(done, 2)
            v.tensor_copy(joint[:, 0, :], T.psum[:, 4, 0:WIDE])
            v.tensor_tensor(joint[:, 1, :], T.psum[:, 5, 0:WIDE], wide[:, 1, :], ALU.add)
            v.drain()
            v.tensor_scalar(scale[:, :, :], joint[:, :, IN:WIDE], 1e-30, None, ALU.max)
            v.drain()
            v.reciprocal(scale[:, :, :], scale[:, :, :])
            v.drain()
            for k in range(2):
                v.tensor_tensor(heads(last_out[:, k, :]), heads(joint[:, k, 0:IN]), last(scale[:, k, :], D), ALU.mult)
            v.drain().then_inc(lasts_made, 1)


class Tables:
    pass


def program(nc, x, src, dst, W0, att0s, att0d, bias, W1, attn_s, attn_d, pos_s, pos_d, out):
    S = Sizes(x, src, W0, att0s, W1, attn_s, pos_s)
    T = Tables()
    h0 = nc.dram_tensor("h0", (S.N, S.IN), F32, kind="Internal").ap()
    x1 = nc.dram_tensor("x1", (S.N + SPARE, S.IN), F32, kind="Internal").ap()
    f1 = nc.dram_tensor("f1", (S.N, S.IN + 2 * S.H1), F32, kind="Internal").ap()
    lists = nc.dram_tensor("lists", ((P + LIST_PADS) * S.W, 3), F32, kind="Internal").ap()
    logits0 = nc.dram_tensor("logits0", (S.N, 2 * S.H0), F32, kind="Internal").ap()
    with ExitStack() as ctx:
        def sb(n, s, d=F32):
            return ctx.enter_context(nc.sbuf_tensor(n, s, d))
        T.psum = ctx.enter_context(nc.psum_tensor("psum", [P, 8, BANK], F32))
        T.src = sb("list_src", [P, S.LW + EDGE_COLS], I32)
        T.dst = sb("list_dst", [P, S.LW + EDGE_COLS], I32)
        T.start = sb("list_start", [P, S.LW + 1])
        T.low_start = sb("list_low_start", [P, S.LW + EDGE_COLS])
        T.keep = sb("list_keep", [P, S.LW])
        T.low_pad = sb("list_low_pad", [P, S.LW + EDGE_COLS])
        T.own = sb("list_own", [P, S.LW])
        T.own_start = sb("list_own_start", [P, S.LW])
        T.low_own = sb("list_low_own", [P, S.LW])
        T.low_own1 = sb("list_low_own1", [P, S.LW + EDGE_COLS])
        T.head_end = sb("list_head_end", [P, S.LW])
        T.out_row = sb("list_out_row", [P, S.LW], I32)
        T.out_row1 = sb("list_out_row1", [P, S.LW], I32)
        T.tail_row = sb("tail_row", [P, 1], I32)
        T.last_row = sb("last_row", [P, 2], I32)
        T.has_head = sb("has_head", [P, 1])
        T.count = sb("count", [P, 1])
        T.trips = sb("trips", [1, 1], I32)
        T.eps = sb("eps", [P, 1])
        T.ident = sb("ident", [P, P])
        T.bias_b = sb("bias_b", [P, S.IN])
        T.w_high = sb("w_high", [P, S.KC, S.H0 * S.C0], F32R)
        T.w_low = sb("w_low", [P, S.KC, S.H0 * S.C0], F32R)
        T.r0 = sb("r0", [P, S.KC, S.IN + 2 * S.H0])
        T.r1 = sb("r1", [P, S.KC, S.IN + 2 * S.H1])
        T.cross = Cross(nc, ctx, "cross0", S.H0)
        T.cross1 = Cross(nc, ctx, "cross1", S.H1, T.cross)
        prepare(nc, S, T, lists, src, dst, W0, att0s, att0d, W1, pos_s, pos_d, bias)
        node_pass(nc, S, T, 0, x, h=h0, rows_out=logits0, base=x1)
        with ExitStack() as inner:
            T.alpha = inner.enter_context(nc.sbuf_tensor("alpha", [P, S.LW, S.H0], F32))
            with ExitStack() as scoring:
                T.score = scoring.enter_context(nc.sbuf_tensor("score", [P, S.LW, S.H0], F32))
                T.score_own = scoring.enter_context(nc.sbuf_tensor("score_own", [P, S.LW, S.H0], F32))
                softmax(nc, S, T, logits0, W0, attn_s, attn_d)
            edge_pass0(nc, S, T, h0, x1)
        node_pass(nc, S, T, 1, x1, rows_out=f1, base=out)
        edge_pass1(nc, S, T, f1, out)


_INS = ['x', 'src', 'dst', 'L0_gnn_W', 'L0_gnn_att_src', 'L0_gnn_att_dst', 'L0_gnn_bias', 'L1_gnn_W',
        'L1_gnn_attn_src', 'L1_gnn_attn_dst', 'L1_gnn_pos_attn_src', 'L1_gnn_pos_attn_dst']


def kernel(**inputs):
    import numpy as _np
    import concourse.bacc as _bacc
    from concourse import mybir as _mybir
    from concourse.bass_utils import run_bass_kernel_spmd as _run

    nc = _bacc.Bacc("TRN2", target_bir_lowering=False, num_devices=1)
    arrays, args = {}, []
    for name in _INS:
        a = _np.ascontiguousarray(inputs[name])
        arrays[f"in_{name}_dram"] = a
        args.append(nc.dram_tensor(f"in_{name}_dram", a.shape, _mybir.dt.from_np(a.dtype), kind="ExternalInput").ap())
    n, c = inputs['x'].shape
    out = nc.dram_tensor("out_0_dram", (n + SPARE, c), _mybir.dt.float32, kind="ExternalOutput").ap()
    program(nc, *args, out)
    r = _run(nc, [arrays], core_ids=[0])
    return r.results[0]["out_0_dram"][:n]
```
